# Optimizing a Trainium2 kernel written in Bass

```python
import numpy as np
import jax
import jax.numpy as jnp

def _softmax(x, axis=-1):
    return jax.nn.softmax(x, axis=axis)

def _gelu(x):
    return jax.nn.gelu(x, approximate=True)

def _silu(x):
    return jax.nn.silu(x)

def _sigmoid(x):
    return jax.nn.sigmoid(x)

def _layernorm(x, axis=-1, eps=1e-05):
    m = jnp.mean(x, axis=axis, keepdims=True)
    v = jnp.var(x, axis=axis, keepdims=True)
    return (x - m) / jnp.sqrt(v + eps)

def _scatter_add(tgt, idx, src, axis=0):
    return tgt.at[idx].add(src)

def _segment_sum(src, seg, n):
    return jax.ops.segment_sum(src, seg, n)
kernel_name = 'mk_dlrm_tower_d1_rec_r8_a5f686'

def setup_inputs(seed: int=0):
    np.random.seed(seed)
    _w = jnp.asarray

    def _rec_inputs():
        import jax
        import jax.numpy as jnp
        _tk = jax.random.key(seed)
        dense_ctx = jax.random.normal(jax.random.fold_in(_tk, 190), (512, 16), jnp.float32)
        ids = jnp.stack([jax.random.randint(jax.random.fold_in(_tk, 200 + f), (512,), 0, v, jnp.int32) for f, v in enumerate([125000, 1250, 12500, 1000, 125000, 1250, 1000, 125000, 12500, 125000, 1000, 12500, 125000, 1000, 1000, 12500, 1000, 125000, 1250, 1000, 125000, 125000, 1000, 1250, 12500, 125000, 1000, 125000, 1000, 125000, 1250, 1250, 1250, 125000, 125000, 125000, 1000, 12500, 12500, 12500, 12500, 1250, 1250, 1250, 1000, 1250, 1000, 1000, 12500, 1000, 1250, 1000, 1000, 1000, 1250, 1000, 12500, 1250, 1000, 12500, 1250, 1250, 12500, 12500])], axis=1)
        tbl_0 = 0.05 * jax.random.normal(jax.random.fold_in(_tk, 500 + 0), (125000, 16), jnp.float32)
        tbl_1 = 0.05 * jax.random.normal(jax.random.fold_in(_tk, 500 + 1), (1250, 16), jnp.float32)
        tbl_2 = 0.05 * jax.random.normal(jax.random.fold_in(_tk, 500 + 2), (12500, 16), jnp.float32)
        tbl_3 = 0.05 * jax.random.normal(jax.random.fold_in(_tk, 500 + 3), (1000, 16), jnp.float32)
        tbl_4 = 0.05 * jax.random.normal(jax.random.fold_in(_tk, 500 + 4), (125000, 16), jnp.float32)
        tbl_5 = 0.05 * jax.random.normal(jax.random.fold_in(_tk, 500 + 5), (1250, 16), jnp.float32)
        tbl_6 = 0.05 * jax.random.normal(jax.random.fold_in(_tk, 500 + 6), (1000, 16), jnp.float32)
        tbl_7 = 0.05 * jax.random.normal(jax.random.fold_in(_tk, 500 + 7), (125000, 16), jnp.float32)
        tbl_8 = 0.05 * jax.random.normal(jax.random.fold_in(_tk, 500 + 8), (12500, 16), jnp.float32)
        tbl_9 = 0.05 * jax.random.normal(jax.random.fold_in(_tk, 500 + 9), (125000, 16), jnp.float32)
        tbl_10 = 0.05 * jax.random.normal(jax.random.fold_in(_tk, 500 + 10), (1000, 16), jnp.float32)
        tbl_11 = 0.05 * jax.random.normal(jax.random.fold_in(_tk, 500 + 11), (12500, 16), jnp.float32)
        tbl_12 = 0.05 * jax.random.normal(jax.random.fold_in(_tk, 500 + 12), (125000, 16), jnp.float32)
        tbl_13 = 0.05 * jax.random.normal(jax.random.fold_in(_tk, 500 + 13), (1000, 16), jnp.float32)
        tbl_14 = 0.05 * jax.random.normal(jax.random.fold_in(_tk, 500 + 14), (1000, 16), jnp.float32)
        tbl_15 = 0.05 * jax.random.normal(jax.random.fold_in(_tk, 500 + 15), (12500, 16), jnp.float32)
        tbl_16 = 0.05 * jax.random.normal(jax.random.fold_in(_tk, 500 + 16), (1000, 16), jnp.float32)
        tbl_17 = 0.05 * jax.random.normal(jax.random.fold_in(_tk, 500 + 17), (125000, 16), jnp.float32)
        tbl_18 = 0.05 * jax.random.normal(jax.random.fold_in(_tk, 500 + 18), (1250, 16), jnp.float32)
        tbl_19 = 0.05 * jax.random.normal(jax.random.fold_in(_tk, 500 + 19), (1000, 16), jnp.float32)
        tbl_20 = 0.05 * jax.random.normal(jax.random.fold_in(_tk, 500 + 20), (125000, 16), jnp.float32)
        tbl_21 = 0.05 * jax.random.normal(jax.random.fold_in(_tk, 500 + 21), (125000, 16), jnp.float32)
        tbl_22 = 0.05 * jax.random.normal(jax.random.fold_in(_tk, 500 + 22), (1000, 16), jnp.float32)
        tbl_23 = 0.05 * jax.random.normal(jax.random.fold_in(_tk, 500 + 23), (1250, 16), jnp.float32)
        tbl_24 = 0.05 * jax.random.normal(jax.random.fold_in(_tk, 500 + 24), (12500, 16), jnp.float32)
        tbl_25 = 0.05 * jax.random.normal(jax.random.fold_in(_tk, 500 + 25), (125000, 16), jnp.float32)
        tbl_26 = 0.05 * jax.random.normal(jax.random.fold_in(_tk, 500 + 26), (1000, 16), jnp.float32)
        tbl_27 = 0.05 * jax.random.normal(jax.random.fold_in(_tk, 500 + 27), (125000, 16), jnp.float32)
        tbl_28 = 0.05 * jax.random.normal(jax.random.fold_in(_tk, 500 + 28), (1000, 16), jnp.float32)
        tbl_29 = 0.05 * jax.random.normal(jax.random.fold_in(_tk, 500 + 29), (125000, 16), jnp.float32)
        tbl_30 = 0.05 * jax.random.normal(jax.random.fold_in(_tk, 500 + 30), (1250, 16), jnp.float32)
        tbl_31 = 0.05 * jax.random.normal(jax.random.fold_in(_tk, 500 + 31), (1250, 16), jnp.float32)
        tbl_32 = 0.05 * jax.random.normal(jax.random.fold_in(_tk, 500 + 32), (1250, 16), jnp.float32)
        tbl_33 = 0.05 * jax.random.normal(jax.random.fold_in(_tk, 500 + 33), (125000, 16), jnp.float32)
        tbl_34 = 0.05 * jax.random.normal(jax.random.fold_in(_tk, 500 + 34), (125000, 16), jnp.float32)
        tbl_35 = 0.05 * jax.random.normal(jax.random.fold_in(_tk, 500 + 35), (125000, 16), jnp.float32)
        tbl_36 = 0.05 * jax.random.normal(jax.random.fold_in(_tk, 500 + 36), (1000, 16), jnp.float32)
        tbl_37 = 0.05 * jax.random.normal(jax.random.fold_in(_tk, 500 + 37), (12500, 16), jnp.float32)
        tbl_38 = 0.05 * jax.random.normal(jax.random.fold_in(_tk, 500 + 38), (12500, 16), jnp.float32)
        tbl_39 = 0.05 * jax.random.normal(jax.random.fold_in(_tk, 500 + 39), (12500, 16), jnp.float32)
        tbl_40 = 0.05 * jax.random.normal(jax.random.fold_in(_tk, 500 + 40), (12500, 16), jnp.float32)
        tbl_41 = 0.05 * jax.random.normal(jax.random.fold_in(_tk, 500 + 41), (1250, 16), jnp.float32)
        tbl_42 = 0.05 * jax.random.normal(jax.random.fold_in(_tk, 500 + 42), (1250, 16), jnp.float32)
        tbl_43 = 0.05 * jax.random.normal(jax.random.fold_in(_tk, 500 + 43), (1250, 16), jnp.float32)
        tbl_44 = 0.05 * jax.random.normal(jax.random.fold_in(_tk, 500 + 44), (1000, 16), jnp.float32)
        tbl_45 = 0.05 * jax.random.normal(jax.random.fold_in(_tk, 500 + 45), (1250, 16), jnp.float32)
        tbl_46 = 0.05 * jax.random.normal(jax.random.fold_in(_tk, 500 + 46), (1000, 16), jnp.float32)
        tbl_47 = 0.05 * jax.random.normal(jax.random.fold_in(_tk, 500 + 47), (1000, 16), jnp.float32)
        tbl_48 = 0.05 * jax.random.normal(jax.random.fold_in(_tk, 500 + 48), (12500, 16), jnp.float32)
        tbl_49 = 0.05 * jax.random.normal(jax.random.fold_in(_tk, 500 + 49), (1000, 16), jnp.float32)
        tbl_50 = 0.05 * jax.random.normal(jax.random.fold_in(_tk, 500 + 50), (1250, 16), jnp.float32)
        tbl_51 = 0.05 * jax.random.normal(jax.random.fold_in(_tk, 500 + 51), (1000, 16), jnp.float32)
        tbl_52 = 0.05 * jax.random.normal(jax.random.fold_in(_tk, 500 + 52), (1000, 16), jnp.float32)
        tbl_53 = 0.05 * jax.random.normal(jax.random.fold_in(_tk, 500 + 53), (1000, 16), jnp.float32)
        tbl_54 = 0.05 * jax.random.normal(jax.random.fold_in(_tk, 500 + 54), (1250, 16), jnp.float32)
        tbl_55 = 0.05 * jax.random.normal(jax.random.fold_in(_tk, 500 + 55), (1000, 16), jnp.float32)
        tbl_56 = 0.05 * jax.random.normal(jax.random.fold_in(_tk, 500 + 56), (12500, 16), jnp.float32)
        tbl_57 = 0.05 * jax.random.normal(jax.random.fold_in(_tk, 500 + 57), (1250, 16), jnp.float32)
        tbl_58 = 0.05 * jax.random.normal(jax.random.fold_in(_tk, 500 + 58), (1000, 16), jnp.float32)
        tbl_59 = 0.05 * jax.random.normal(jax.random.fold_in(_tk, 500 + 59), (12500, 16), jnp.float32)
        tbl_60 = 0.05 * jax.random.normal(jax.random.fold_in(_tk, 500 + 60), (1250, 16), jnp.float32)
        tbl_61 = 0.05 * jax.random.normal(jax.random.fold_in(_tk, 500 + 61), (1250, 16), jnp.float32)
        tbl_62 = 0.05 * jax.random.normal(jax.random.fold_in(_tk, 500 + 62), (12500, 16), jnp.float32)
        tbl_63 = 0.05 * jax.random.normal(jax.random.fold_in(_tk, 500 + 63), (12500, 16), jnp.float32)
        _rk = jax.random.fold_in(_tk, 7)
        W_top1 = 0.05 * jax.random.normal(jax.random.fold_in(_tk, 801), (400, 512), jnp.float32)
        W_top2 = 0.0441942 * jax.random.normal(jax.random.fold_in(_tk, 802), (512, 256), jnp.float32)
        W_top3 = 0.0625 * jax.random.normal(jax.random.fold_in(_tk, 803), (256, 1), jnp.float32)
        b_top1 = jnp.zeros((512,), jnp.float32)
        b_top2 = jnp.zeros((256,), jnp.float32)
        return (dense_ctx, ids, tbl_0, tbl_1, tbl_2, tbl_3, tbl_4, tbl_5, tbl_6, tbl_7, tbl_8, tbl_9, tbl_10, tbl_11, tbl_12, tbl_13, tbl_14, tbl_15, tbl_16, tbl_17, tbl_18, tbl_19, tbl_20, tbl_21, tbl_22, tbl_23, tbl_24, tbl_25, tbl_26, tbl_27, tbl_28, tbl_29, tbl_30, tbl_31, tbl_32, tbl_33, tbl_34, tbl_35, tbl_36, tbl_37, tbl_38, tbl_39, tbl_40, tbl_41, tbl_42, tbl_43, tbl_44, tbl_45, tbl_46, tbl_47, tbl_48, tbl_49, tbl_50, tbl_51, tbl_52, tbl_53, tbl_54, tbl_55, tbl_56, tbl_57, tbl_58, tbl_59, tbl_60, tbl_61, tbl_62, tbl_63, W_top1, b_top1, W_top2, b_top2, W_top3)
    dense_ctx, ids, tbl_0, tbl_1, tbl_2, tbl_3, tbl_4, tbl_5, tbl_6, tbl_7, tbl_8, tbl_9, tbl_10, tbl_11, tbl_12, tbl_13, tbl_14, tbl_15, tbl_16, tbl_17, tbl_18, tbl_19, tbl_20, tbl_21, tbl_22, tbl_23, tbl_24, tbl_25, tbl_26, tbl_27, tbl_28, tbl_29, tbl_30, tbl_31, tbl_32, tbl_33, tbl_34, tbl_35, tbl_36, tbl_37, tbl_38, tbl_39, tbl_40, tbl_41, tbl_42, tbl_43, tbl_44, tbl_45, tbl_46, tbl_47, tbl_48, tbl_49, tbl_50, tbl_51, tbl_52, tbl_53, tbl_54, tbl_55, tbl_56, tbl_57, tbl_58, tbl_59, tbl_60, tbl_61, tbl_62, tbl_63, W_top1, b_top1, W_top2, b_top2, W_top3 = _rec_inputs()

    def _L0_rec_setup():
        import jax, jax.numpy as jnp
        import numpy as np
        BATCH, FIELDS, EMBED = (256, 64, 16)
        LAYERS = [128, 128, 128]
        key = jax.random.key(seed)
        ks = jax.random.split(key, 7)
        inp = {'input': jax.random.normal(ks[0], (BATCH, FIELDS, EMBED), dtype=jnp.float32)}
        in_ch = [FIELDS * FIELDS, FIELDS * LAYERS[0], FIELDS * LAYERS[1]]
        for i, (cin, cout) in enumerate(zip(in_ch, LAYERS)):
            scale = 1.0 / np.sqrt(cin)
            inp[f'W{i}'] = jax.random.uniform(ks[1 + 2 * i], (cout, cin), jnp.float32, -scale, scale)
            inp[f'b{i}'] = jax.random.uniform(ks[2 + 2 * i], (cout,), jnp.float32, -scale, scale)
        return inp
    _L0_rec_all = _L0_rec_setup()
    _L0_rec_in = {k: v for k, v in _L0_rec_all.items() if k in ('W0', 'b0', 'W1', 'b1', 'W2', 'b2')}
    del _L0_rec_all
    return {'dense_ctx': dense_ctx, 'ids': ids, 'tbl_0': tbl_0, 'tbl_1': tbl_1, 'tbl_2': tbl_2, 'tbl_3': tbl_3, 'tbl_4': tbl_4, 'tbl_5': tbl_5, 'tbl_6': tbl_6, 'tbl_7': tbl_7, 'tbl_8': tbl_8, 'tbl_9': tbl_9, 'tbl_10': tbl_10, 'tbl_11': tbl_11, 'tbl_12': tbl_12, 'tbl_13': tbl_13, 'tbl_14': tbl_14, 'tbl_15': tbl_15, 'tbl_16': tbl_16, 'tbl_17': tbl_17, 'tbl_18': tbl_18, 'tbl_19': tbl_19, 'tbl_20': tbl_20, 'tbl_21': tbl_21, 'tbl_22': tbl_22, 'tbl_23': tbl_23, 'tbl_24': tbl_24, 'tbl_25': tbl_25, 'tbl_26': tbl_26, 'tbl_27': tbl_27, 'tbl_28': tbl_28, 'tbl_29': tbl_29, 'tbl_30': tbl_30, 'tbl_31': tbl_31, 'tbl_32': tbl_32, 'tbl_33': tbl_33, 'tbl_34': tbl_34, 'tbl_35': tbl_35, 'tbl_36': tbl_36, 'tbl_37': tbl_37, 'tbl_38': tbl_38, 'tbl_39': tbl_39, 'tbl_40': tbl_40, 'tbl_41': tbl_41, 'tbl_42': tbl_42, 'tbl_43': tbl_43, 'tbl_44': tbl_44, 'tbl_45': tbl_45, 'tbl_46': tbl_46, 'tbl_47': tbl_47, 'tbl_48': tbl_48, 'tbl_49': tbl_49, 'tbl_50': tbl_50, 'tbl_51': tbl_51, 'tbl_52': tbl_52, 'tbl_53': tbl_53, 'tbl_54': tbl_54, 'tbl_55': tbl_55, 'tbl_56': tbl_56, 'tbl_57': tbl_57, 'tbl_58': tbl_58, 'tbl_59': tbl_59, 'tbl_60': tbl_60, 'tbl_61': tbl_61, 'tbl_62': tbl_62, 'tbl_63': tbl_63, 'W_top1': W_top1, 'b_top1': b_top1, 'W_top2': W_top2, 'b_top2': b_top2, 'W_top3': W_top3, 'L0_rec_W0': _L0_rec_in['W0'], 'L0_rec_b0': _L0_rec_in['b0'], 'L0_rec_W1': _L0_rec_in['W1'], 'L0_rec_b1': _L0_rec_in['b1'], 'L0_rec_W2': _L0_rec_in['W2'], 'L0_rec_b2': _L0_rec_in['b2']}

def reference(dense_ctx, ids, tbl_0, tbl_1, tbl_2, tbl_3, tbl_4, tbl_5, tbl_6, tbl_7, tbl_8, tbl_9, tbl_10, tbl_11, tbl_12, tbl_13, tbl_14, tbl_15, tbl_16, tbl_17, tbl_18, tbl_19, tbl_20, tbl_21, tbl_22, tbl_23, tbl_24, tbl_25, tbl_26, tbl_27, tbl_28, tbl_29, tbl_30, tbl_31, tbl_32, tbl_33, tbl_34, tbl_35, tbl_36, tbl_37, tbl_38, tbl_39, tbl_40, tbl_41, tbl_42, tbl_43, tbl_44, tbl_45, tbl_46, tbl_47, tbl_48, tbl_49, tbl_50, tbl_51, tbl_52, tbl_53, tbl_54, tbl_55, tbl_56, tbl_57, tbl_58, tbl_59, tbl_60, tbl_61, tbl_62, tbl_63, W_top1, b_top1, W_top2, b_top2, W_top3, L0_rec_W0, L0_rec_b0, L0_rec_W1, L0_rec_b1, L0_rec_W2, L0_rec_b2):
    import jax
    import jax.numpy as jnp

    def _L0_rec_ref(input, W0, b0, W1, b1, W2, b2):
        import jax, jax.numpy as jnp
        import numpy as np
        BATCH, FIELDS, EMBED = (256, 64, 16)
        LAYERS = [128, 128, 128]
        params = [(W0, b0), (W1, b1), (W2, b2)]
        x_vec = input
        outs = []
        for W, b in params:
            z = jnp.einsum('bhd,bfd->bhfd', x_vec, input)
            B, h, f, d = z.shape
            z = z.reshape(B, h * f, d)
            x_vec = jnp.einsum('oc,bcd->bod', W, z) + b[None, :, None]
            outs.append(x_vec.sum(axis=2))
        return jnp.concatenate(outs, axis=1)
    e = jnp.stack([tbl_0[ids[:, 0]], tbl_1[ids[:, 1]], tbl_2[ids[:, 2]], tbl_3[ids[:, 3]], tbl_4[ids[:, 4]], tbl_5[ids[:, 5]], tbl_6[ids[:, 6]], tbl_7[ids[:, 7]], tbl_8[ids[:, 8]], tbl_9[ids[:, 9]], tbl_10[ids[:, 10]], tbl_11[ids[:, 11]], tbl_12[ids[:, 12]], tbl_13[ids[:, 13]], tbl_14[ids[:, 14]], tbl_15[ids[:, 15]], tbl_16[ids[:, 16]], tbl_17[ids[:, 17]], tbl_18[ids[:, 18]], tbl_19[ids[:, 19]], tbl_20[ids[:, 20]], tbl_21[ids[:, 21]], tbl_22[ids[:, 22]], tbl_23[ids[:, 23]], tbl_24[ids[:, 24]], tbl_25[ids[:, 25]], tbl_26[ids[:, 26]], tbl_27[ids[:, 27]], tbl_28[ids[:, 28]], tbl_29[ids[:, 29]], tbl_30[ids[:, 30]], tbl_31[ids[:, 31]], tbl_32[ids[:, 32]], tbl_33[ids[:, 33]], tbl_34[ids[:, 34]], tbl_35[ids[:, 35]], tbl_36[ids[:, 36]], tbl_37[ids[:, 37]], tbl_38[ids[:, 38]], tbl_39[ids[:, 39]], tbl_40[ids[:, 40]], tbl_41[ids[:, 41]], tbl_42[ids[:, 42]], tbl_43[ids[:, 43]], tbl_44[ids[:, 44]], tbl_45[ids[:, 45]], tbl_46[ids[:, 46]], tbl_47[ids[:, 47]], tbl_48[ids[:, 48]], tbl_49[ids[:, 49]], tbl_50[ids[:, 50]], tbl_51[ids[:, 51]], tbl_52[ids[:, 52]], tbl_53[ids[:, 53]], tbl_54[ids[:, 54]], tbl_55[ids[:, 55]], tbl_56[ids[:, 56]], tbl_57[ids[:, 57]], tbl_58[ids[:, 58]], tbl_59[ids[:, 59]], tbl_60[ids[:, 60]], tbl_61[ids[:, 61]], tbl_62[ids[:, 62]], tbl_63[ids[:, 63]]], axis=1)
    z = _L0_rec_ref(e, L0_rec_W0, L0_rec_b0, L0_rec_W1, L0_rec_b1, L0_rec_W2, L0_rec_b2)
    z = z.reshape(z.shape[0], -1)
    h = jnp.concatenate([z, dense_ctx], axis=1)
    h = jnp.maximum(h @ W_top1 + b_top1, 0.0)
    h = jnp.maximum(h @ W_top2 + b_top2, 0.0)
    y = h @ W_top3
    return y

_drawn_inputs = setup_inputs


def setup_inputs(seed=0):
    import zlib

    import numpy as np

    out = dict(_drawn_inputs(seed))
    spreads = {'b_top1': (0.0, 0.1), 'b_top2': (0.0, 0.1)}
    factors = {'tbl_0': 8.0,
     'tbl_1': 8.0,
     'tbl_2': 8.0,
     'tbl_3': 8.0,
     'tbl_4': 8.0,
     'tbl_5': 8.0,
     'tbl_6': 8.0,
     'tbl_7': 8.0,
     'tbl_8': 8.0,
     'tbl_9': 8.0,
     'tbl_10': 8.0,
     'tbl_11': 8.0,
     'tbl_12': 8.0,
     'tbl_13': 8.0,
     'tbl_14': 8.0,
     'tbl_15': 8.0,
     'tbl_16': 8.0,
     'tbl_17': 8.0,
     'tbl_18': 8.0,
     'tbl_19': 8.0,
     'tbl_20': 8.0,
     'tbl_21': 8.0,
     'tbl_22': 8.0,
     'tbl_23': 8.0,
     'tbl_24': 8.0,
     'tbl_25': 8.0,
     'tbl_26': 8.0,
     'tbl_27': 8.0,
     'tbl_28': 8.0,
     'tbl_29': 8.0,
     'tbl_30': 8.0,
     'tbl_31': 8.0,
     'tbl_32': 8.0,
     'tbl_33': 8.0,
     'tbl_34': 8.0,
     'tbl_35': 8.0,
     'tbl_36': 8.0,
     'tbl_37': 8.0,
     'tbl_38': 8.0,
     'tbl_39': 8.0,
     'tbl_40': 8.0,
     'tbl_41': 8.0,
     'tbl_42': 8.0,
     'tbl_43': 8.0,
     'tbl_44': 8.0,
     'tbl_45': 8.0,
     'tbl_46': 8.0,
     'tbl_47': 8.0,
     'tbl_48': 8.0,
     'tbl_49': 8.0,
     'tbl_50': 8.0,
     'tbl_51': 8.0,
     'tbl_52': 8.0,
     'tbl_53': 8.0,
     'tbl_54': 8.0,
     'tbl_55': 8.0,
     'tbl_56': 8.0,
     'tbl_57': 8.0,
     'tbl_58': 8.0,
     'tbl_59': 8.0,
     'tbl_60': 8.0,
     'tbl_61': 8.0,
     'tbl_62': 8.0,
     'tbl_63': 8.0,
     'L0_rec_W1': 8.0,
     'L0_rec_W2': 8.0}
    for name, (base, spread) in spreads.items():
        noise = np.random.default_rng([zlib.crc32(name.encode()), seed]).standard_normal(out[name].shape)
        drawn = base * np.exp(spread * noise) if base else spread * noise
        out[name] = jnp.asarray(drawn.astype(out[name].dtype))
    for name, factor in factors.items():
        out[name] = (out[name] * factor).astype(out[name].dtype)
    return out
```

```python
from contextlib import ExitStack

import concourse.bass as bass
from concourse import mybir

ALU = mybir.AluOpType
ACT = mybir.ActivationFunctionType
AX = mybir.AxisListType
F32 = mybir.dt.float32
I32 = mybir.dt.int32
U32 = mybir.dt.uint32

P = 128
BATCH, FIELDS, EMBED, MAPS = 512, 64, 16, 128
HID1, HID2 = 512, 256
BB = P
NBB = BATCH // BB
COLS = 512
CB = COLS // EMBED
PER = BB // CB
NCB = BATCH // CB
HT, FT = 16, 8
NI0, NI1, NJ = FIELDS // HT, MAPS // HT, FIELDS // FT
GROUP = 4
RING = 2
W2_PIECE, W2_RING = 4, 4
NP = FIELDS // W2_PIECE
NCH = COLS // P
X0_DMAS = NJ + NI0
X1_DMAS = NI1 // 2
DPG = 4
NX = EMBED // DPG

L1_GROUPS = [(0, 0, 4), (0, 4, 4), (1, 2, 2), (1, 4, 4), (2, 4, 4), (3, 6, 2)]
L1_TILES = [(i, j) for i in range(NI0) for j in range(2 * i, NJ)]
L2_HALF = [[(i, j, GROUP) for i in range(s * NI1 // 2, (s + 1) * NI1 // 2) for j in range(0, NJ, GROUP)]
           for s in range(2)]
NA, NB = len(L2_HALF[0]), len(L1_GROUPS)
NG = 2 * NA + NB
assert NG % RING == 0 and NB % RING == 0 and NP % W2_RING == 0


def groups_before(c):
    return NG * c + NB


def x0_copied(t):
    return 12 * t + 1


class TransposeBank:

    def __init__(self, t, k, c):
        self.has_x0 = k == 2 and not isinstance(c, int)
        self.has_x0d = not (isinstance(c, int) and c + 2 >= NCB)
        self.has_x2t = not (isinstance(c, int) and c == 0)
        if isinstance(c, int) and c >= NCB - 1:
            first = 12 * (NBB - 1) + 10 + (c - NCB + 1)
        elif k == 0:
            first = NX + 2
        else:
            first = 12 * t + (0, 7, 9, 15, 17)[k]
        self.x0 = first
        self.x0d = first + NX * self.has_x0
        self.x2t = self.x0d + self.has_x0d


def repeat_each(rows, n):
    (step, r), (cs, cols) = rows.ap
    return bass.AP(rows.tensor, rows.offset, [[step, r], [0, n], [cs, cols]])


def repeat_set(rows, n):
    (step, r), (cs, cols) = rows.ap
    return bass.AP(rows.tensor, rows.offset, [[0, n], [step, r], [cs, cols]])


def dlrm_tower(nc, ins, tables, out):
    with ExitStack() as ctx:
        def sb(name, shape, dt=F32):
            return ctx.enter_context(nc.sbuf_tensor(name, shape, dt))

        def ps(name, shape):
            return ctx.enter_context(nc.psum_tensor(name, shape, F32))

        def sem(name):
            return ctx.enter_context(nc.semaphore(name))

        w0 = sb("w0", [P, len(L1_TILES), P])
        w1 = sb("w1", [P, NI1 * NJ, P])
        w2 = sb("w2", [P, W2_RING, W2_PIECE, P])
        wt1 = sb("wt1", [P, 4, HID1])
        wt2 = sb("wt2", [P, HID1 // P, HID2])
        wt3 = sb("wt3", [P, HID2 // P])
        cin_bias = sb("cin_bias", [P, 3])
        bias3_sum = sb("bias3_sum", [P, 1])
        bt1 = sb("bt1", [P, HID1 // P])
        bt2 = sb("bt2", [P, HID2 // P])
        ident = sb("ident", [P, P])
        pair_mask = sb("pair_mask", [P, 2])
        ids = sb("ids", [P, NBB, FIELDS], I32)
        emb = sb("emb", [P, FIELDS, EMBED])
        x0 = sb("x0", [FIELDS, BB, EMBED])
        x0f = sb("x0f", [P, 2, NJ, COLS])
        x0h = sb("x0h", [P, NI0, COLS])
        x1 = sb("x1", [P, COLS])
        x1h = sb("x1h", [P, NI1, COLS])
        prod = sb("prod", [P, RING, GROUP, COLS])
        x2 = sb("x2", [P, COLS])
        x2t = sb("x2t", [P, NCH, MAPS])
        x0d = sb("x0d", [P, PER, NCH, 2, FIELDS])
        gram = sb("gram", [P, FIELDS, BB])
        sums = sb("sums", [P, 3, BATCH])
        dense = sb("dense", [EMBED, BATCH])
        hid1 = x0f[:, 0, 0:4, :]
        hid2 = x0f[:, 0, 4:6, :]
        y = x0f[:, 0, 6, :]
        w0_other = prod[:, 0, :, :].rearrange("p g n -> p (g n)")

        x0_dram = nc.dram_tensor("x0_dram", (NBB, FIELDS, BB * EMBED), F32, kind="Internal").ap()

        l1_ps = ps("l1_ps", [P, COLS])
        l2_ps = ps("l2_ps", [P, 2, COLS])
        t_ps = ps("t_ps", [P, COLS])
        g_ps = ps("g_ps", [P, 4, COLS])

        ids_in, ident_in, mask_in, bias_in = sem("ids_in"), sem("ident_in"), sem("mask_in"), sem("bias_in")
        w0_in, w0_folded, w1_in, mlp_in = sem("w0_in"), sem("w0_folded"), sem("w1_in"), sem("mlp_in")
        gathered = sem("gathered")
        bank_filled, bank_copied = sem("bank_filled"), sem("bank_copied")
        x0_stored, x0_in = sem("x0_stored"), sem("x0_in")
        x1h_in = [sem("x1h_in_first"), sem("x1h_in_second")]
        prod_ready, prod_used = sem("prod_ready"), sem("prod_used")
        x1_ready, x2_ready = sem("x1_ready"), sem("x2_ready")
        sum1_done, sum2_done = sem("sum1_done"), sem("sum2_done")
        sum3_done = sem("sum3_done")
        gram_ps_done, gram_copied = sem("gram_ps_done"), sem("gram_copied")
        w2_in = [sem(f"w2_in{r}") for r in range(W2_RING)]
        w2_used = sem("w2_used")
        mlp_ps_done, mlp_ready = sem("mlp_ps_done"), sem("mlp_ready")
        out_written = sem("out_written")

        def walk(eng, step):
            step(0, 0, 0)
            with eng.Fori(0, NBB - 1) as t:
                for k in range(1, PER + 1):
                    step(t, k, t * PER + k)
            for k in range(1, PER):
                step(NBB - 1, k, PER * (NBB - 1) + k)

        def is_step(c, n):
            return isinstance(c, int) and c == n

        block = ctx.enter_context(nc.Block())

        @block.gpsimd
        def _(pool):
            pool.wait_ge(ids_in, 16)
            for t in range(NBB):
                if t:
                    pool.wait_ge(bank_copied, NX if t == 1 else x0_copied(t - 1))
                for f in range(FIELDS):
                    nc.gpsimd.indirect_dma_start(
                        out=emb[:, f, :], out_offset=None, in_=tables[f],
                        in_offset=bass.IndirectOffsetOnAxis(ap=ids[:, t, f:f + 1].bitcast(U32), axis=0),
                    ).then_inc(gathered, 16)
                pool.wait_ge(gathered, 16 * FIELDS * (t + 1))

        @block.sync
        def _(sp):
            sp.dma_start(ids[:, :, :], ins["ids"].rearrange("(t p) f -> p t f", p=P)).then_inc(ids_in, 16)
            sp.dma_start(ident[:, :], ins["ident"]).then_inc(ident_in, 16)
            sp.dma_start(pair_mask[:, :], ins["pair_mask"]).then_inc(mask_in, 16)
            n = 0
            for i in range(NI0):
                m = NJ - 2 * i
                sp.dma_start(w0[:, n:n + m, :], ins["w0_hf"][:, i, 2 * i:NJ, :]).then_inc(w0_in, 16)
                n += m
            n = 0
            for i in range(NI0 - 1):
                m = NJ - 2 * i - 2
                sp.dma_start(w0_other[:, n * P:(n + m) * P].rearrange("p (m o) -> p m o", o=P),
                             ins["w0_fh"][:, i, 2 * i + 2:NJ, :]).then_inc(w0_in, 16)
                n += m
            sp.dma_start(cin_bias[:, :], ins["cin_bias"]).then_inc(bias_in, 16)
            sp.dma_start(w1[:, :, :], ins["w1"]).then_inc(w1_in, 16)

            def store_x0(t):
                sp.dma_start(x0_dram[t], x0[:, :, :].rearrange("f b d -> f (b d)")).then_inc(x0_stored, 16)

            def load_x0(t, q, b):
                rows = x0_dram[t, :, q * COLS:(q + 1) * COLS]
                for j in range(NJ):
                    sp.dma_start(x0f[:, b, j, :], repeat_set(rows[FT * j:FT * (j + 1), :], HT)).then_inc(x0_in, 16)
                for i in range(NI0):
                    sp.dma_start(x0h[:, i, :], repeat_each(rows[HT * i:HT * (i + 1), :], FT)).then_inc(x0_in, 16)

            def load_x1(half):
                for i in range(half * NI1 // 2, (half + 1) * NI1 // 2):
                    sp.dma_start(x1h[:, i, :], repeat_each(x1[HT * i:HT * (i + 1), :], FT)).then_inc(x1h_in[half], 16)

            def load_w2(n):
                sp.dma_start(w2[:, n % W2_RING, :, :],
                             ins["w2"][:, n * W2_PIECE:(n + 1) * W2_PIECE, :]).then_inc(w2_in[n % W2_RING], 16)

            sp.wait_ge(bank_copied, NX)
            store_x0(0)
            sp.wait_ge(x0_stored, 16)
            load_x0(0, 0, 0)
            for n in range(W2_RING):
                load_w2(n)
            sp.dma_start(wt1[:, 0:3, :], ins["wt1"][0:3 * P, :].rearrange("(k p) n -> p k n", p=P)).then_inc(mlp_in, 16)
            sp.dma_start(wt1[0:EMBED, 3, :], ins["wt1"][3 * P:3 * P + EMBED, :]).then_inc(mlp_in, 16)
            sp.dma_start(wt2[:, :, :], ins["wt2"].rearrange("(k p) n -> p k n", p=P)).then_inc(mlp_in, 16)
            sp.dma_start(wt3[:, :], ins["wt3"]).then_inc(mlp_in, 16)
            sp.dma_start(bt1[:, :], ins["bt1"]).then_inc(mlp_in, 16)
            sp.dma_start(bt2[:, :], ins["bt2"]).then_inc(mlp_in, 16)
            sp.dma_start(dense[:, :], ins["dense"]).then_inc(mlp_in, 16)
            sp.wait_ge(x1_ready, 1)
            load_x1(0)

            def step(t, k, c):
                sp.wait_ge(prod_ready, groups_before(c))
                load_x1(1)
                if is_step(c, NCB - 1):
                    return
                if k == PER - 1:
                    sp.wait_ge(x0_stored, 16 * (t + 2))
                load_x0(t + (k + 1) // PER, (k + 1) % PER, (k + 1) % 2)
                if TransposeBank(t, k, c).has_x0:
                    sp.wait_ge(bank_copied, x0_copied(t + 1))
                    store_x0(t + 1)
                sp.wait_ge(x1_ready, c + 2)
                load_x1(0)
                if k == PER:
                    for n in range(NP):
                        sp.wait_ge(w2_used, t * NP + n + 1)
                        load_w2((n + W2_RING) % NP)

            walk(sp, step)
            for n in range(NP - W2_RING):
                sp.wait_ge(w2_used, (NBB - 1) * NP + n + 1)
                load_w2(n + W2_RING)
            sp.wait_ge(mlp_ready, 7)
            sp.dma_start(out.rearrange("b a -> a b"), y[0:1, :]).then_inc(out_written, 16)
            sp.wait_ge(out_written, 16)

        @block.vector
        def _(dve):
            dve.wait_ge(w0_in, 16 * (2 * NI0 - 1))
            n, m = 0, 0
            for i in range(NI0):
                folded = NJ - 2 * i - 2
                if folded:
                    tiles = w0[:, n + 2:n + 2 + folded, :]
                    nc.vector.tensor_tensor(tiles, tiles, w0_other[:, m * P:(m + folded) * P].rearrange(
                        "p (m o) -> p m o", o=P), ALU.add).then_inc(w0_folded, 1)
                n += folded + 2
                m += folded
            dve.wait_ge(w0_folded, NI0 - 1)

            def product(g, slot, left, right, n):
                if not (isinstance(g, int) and g < RING):
                    dve.wait_ge(prod_used, g - (RING - 1))
                nc.vector.tensor_tensor(prod[:, slot, 0:n, :], left.unsqueeze(1).to_broadcast([P, n, COLS]),
                                        right, ALU.mult).then_inc(prod_ready, 1)

            def layer1_product(g0, x, b):
                i, j, n = L1_GROUPS[x]
                product(g0 + x, x % RING, x0h[:, i, :], x0f[:, b, j:j + n, :], n)

            def layer2_product(g0, half, x, b):
                i, j, n = L2_HALF[half][x]
                product(g0 + x, x % RING, x1h[:, i, :], x0f[:, b, j:j + n, :], n)

            def x0_diagonal(q):
                nc.vector.tensor_tensor(
                    x0d[:, q, :, :, :],
                    t_ps[:, 0:NCH * FIELDS].rearrange("p (n f) -> p n f", f=FIELDS).unsqueeze(2).to_broadcast(
                        [P, NCH, 2, FIELDS]),
                    pair_mask[:, :].unsqueeze(1).unsqueeze(3).to_broadcast([P, NCH, 2, FIELDS]),
                    ALU.mult).then_inc(bank_copied, 1)

            def sum_dims(x, layer, c, done):
                nc.vector.tensor_reduce(sums[:, layer, bass.ds(c * CB, CB)],
                                        x[:, :].rearrange("p (b d) -> p b d", d=EMBED), AX.X, ALU.add).then_inc(done, 1)

            dve.wait_ge(mask_in, 16)
            for q in range(2):
                dve.wait_ge(bank_filled, NX + q + 1)
                x0_diagonal(q)
            dve.wait_ge(x0_in, 16 * X0_DMAS)
            for x in range(NB):
                layer1_product(0, x, 0)
            dve.wait_ge(x1_ready, 1)
            sum_dims(x1, 0, 0, sum1_done)

            def step(t, k, c):
                bank = TransposeBank(t, k, c)
                g0 = groups_before(c)
                dve.wait_ge(x1h_in[0], 16 * X1_DMAS * (c + 1))
                for x in range(NA):
                    layer2_product(g0, 0, x, k % 2)
                if not is_step(c, NCB - 1):
                    dve.wait_ge(x0_in, 16 * X0_DMAS * (c + 2))
                    for x in range(NB):
                        layer1_product(g0 + NA, x, (k + 1) % 2)
                        if x == 1 and bank.has_x0d:
                            dve.wait_ge(bank_filled, bank.x0d + 1)
                            x0_diagonal((k + 2) % PER)
                        if x == 3 and k >= 1:
                            dve.wait_ge(x2_ready, c)
                            sum_dims(x2, 1, c - 1, sum2_done)
                elif True:
                    dve.wait_ge(x2_ready, c)
                    sum_dims(x2, 1, c - 1, sum2_done)
                g1 = g0 + NA + NB * (not is_step(c, NCB - 1))
                dve.wait_ge(x1h_in[1], 16 * X1_DMAS * (c + 1))
                for x in range(NA):
                    layer2_product(g1, 1, x, k % 2)
                    if x == 2 and not is_step(c, NCB - 1):
                        dve.wait_ge(x1_ready, c + 2)
                        sum_dims(x1, 0, c + 1, sum1_done)

            walk(dve, step)
            dve.wait_ge(x2_ready, NCB)
            sum_dims(x2, 1, NCB - 1, sum2_done)

        @block.scalar
        def _(act):
            act.wait_ge(bias_in, 16)
            nc.scalar.mul(bias3_sum[:, :], cin_bias[:, 2:3], float(EMBED)).then_inc(sum3_done, 1)

            def copy_x0(first):
                for n in range(NX):
                    act.wait_ge(bank_filled, first + n + 1)
                    nc.scalar.activation(
                        x0[:, :, n * DPG:(n + 1) * DPG].rearrange("f b d -> f d b"),
                        t_ps[0:FIELDS, :].rearrange("f (d b) -> f d b", d=DPG), ACT.Copy).then_inc(bank_copied, 1)

            def store_x1(used):
                act.wait_ge(prod_used, used)
                nc.scalar.activation(x1[:, :], l1_ps[:, :], ACT.Identity, bias=cin_bias[:, 0:1]).then_inc(x1_ready, 1)

            def store_gram(t, k, c, bank):
                act.wait_ge(bank_filled, bank.x2t + 1)
                nc.scalar.activation(x2t[:, :, :].rearrange("p n h -> p (n h)"), t_ps[:, :],
                                     ACT.Copy).then_inc(bank_copied, 1)
                act.wait_ge(gram_ps_done, c + 1)
                for r in range(4):
                    b = gram[:, :, k * CB:(k + 1) * CB].rearrange("h f (n r a) -> h r n a f", n=NCH, r=4)[:, r]
                    nc.scalar.activation(b, g_ps[:, r, :].rearrange("h (n a f) -> h n a f", n=NCH, a=2),
                                         ACT.Copy).then_inc(gram_copied, 1)

            def store_sum3(t):
                act.wait_ge(sum3_done, t + 1)
                act.wait_ge(w2_used, NP * t + NP)
                nc.scalar.activation(sums[:, 2, bass.ds(t * BB, BB)], l1_ps[:, 0:BB], ACT.Identity,
                                     bias=bias3_sum[:, 0:1]).then_inc(sum3_done, 1)

            copy_x0(0)
            store_x1(NB)

            def step(t, k, c):
                bank = TransposeBank(t, k, c)
                not_last = not is_step(c, NCB - 1)
                if bank.has_x0:
                    act.wait_ge(x0_stored, 16 * (t + 1))
                    copy_x0(bank.x0)
                if not_last:
                    for half in range(2):
                        act.wait_ge(x1h_in[half], 16 * X1_DMAS * (c + 1))
                    act.wait_ge(sum1_done, c + 1)
                    store_x1(groups_before(c) + NA + NB)
                if k >= 1:
                    store_gram(t, (k - 1) % PER, c - 1, bank)
                    act.wait_ge(sum2_done, c)
                act.wait_ge(prod_used, groups_before(c) + 2 * NA + NB * not_last)
                nc.scalar.activation(x2[:, :], l2_ps[:, k % 2, :], ACT.Identity,
                                     bias=cin_bias[:, 1:2]).then_inc(x2_ready, 1)
                if k == PER:
                    store_sum3(t)

            walk(act, step)
            store_gram(NBB - 1, PER - 1, NCB - 1, TransposeBank(NBB, 0, NCB))
            store_sum3(NBB - 1)
            act.wait_ge(mlp_in, 16 * 7)
            for m in range(HID1 // P):
                act.wait_ge(mlp_ps_done, m + 1)
                nc.scalar.activation(hid1[:, m, :], g_ps[:, m, :], ACT.Relu, bias=bt1[:, m:m + 1]).then_inc(mlp_ready, 1)
            for m in range(HID2 // P):
                act.wait_ge(mlp_ps_done, HID1 // P + m + 1)
                nc.scalar.activation(hid2[:, m, :], l2_ps[:, m, :], ACT.Relu, bias=bt2[:, m:m + 1]).then_inc(mlp_ready, 1)
            act.wait_ge(mlp_ps_done, HID1 // P + HID2 // P + 1)
            nc.scalar.activation(y[0:1, :], t_ps[0:1, :], ACT.Copy).then_inc(mlp_ready, 1)

        @block.tensor
        def _(pe):
            def wait_bank(n):
                if not (isinstance(n, int) and n == 0):
                    pe.wait_ge(bank_copied, n)

            def turn(to, rows, n):
                unit = ident[0:rows.partition_size(), 0:rows.partition_size()]
                if n == 0:
                    return nc.tensor.matmul(to, rows, unit, start=True, stop=True)
                return nc.tensor.transpose(to, rows, unit)

            def transpose_x0(first):
                for n in range(NX):
                    wait_bank(first + n)
                    for e in range(DPG):
                        mm = turn(t_ps[0:FIELDS, e * BB:(e + 1) * BB], emb[:, :, n * DPG + e], e)
                    mm.then_inc(bank_filled, 1)

            def transpose_x0d(index, q):
                wait_bank(index)
                rows = x0[:, q * CB:(q + 1) * CB, :].rearrange("f b d -> f (b d)")
                for n in range(NCH):
                    mm = turn(t_ps[:, n * FIELDS:(n + 1) * FIELDS], rows[:, n * P:(n + 1) * P], n)
                mm.then_inc(bank_filled, 1)

            def contract(g, slot, acc, weights, tiles, start, stop):
                pe.wait_ge(prod_ready, g + 1)
                for n, tile in enumerate(tiles):
                    mm = nc.tensor.matmul(acc, weights[:, tile, :], prod[:, slot, n, :],
                                          start=start and n == 0, stop=stop and n == len(tiles) - 1)
                mm.then_inc(prod_used, 1)

            def layer1(g0):
                for x, (i, j, n) in enumerate(L1_GROUPS):
                    at = L1_TILES.index((i, j))
                    contract(g0 + x, x % RING, l1_ps[:, :], w0, range(at, at + n), x == 0, x == NB - 1)

            def layer2(g0, half, b):
                for x, (i, j, n) in enumerate(L2_HALF[half]):
                    contract(g0 + x, x % RING, l2_ps[:, b, :], w1, range(i * NJ + j, i * NJ + j + n),
                             half == 0 and x == 0, half == 1 and x == NA - 1)

            def make_gram(c, q, bank):
                pe.wait_ge(x2_ready, c + 1)
                wait_bank(bank.x2t)
                for n in range(NCH):
                    mm = nc.tensor.transpose(t_ps[:, n * P:(n + 1) * P], x2[:, n * P:(n + 1) * P], ident[:, :])
                mm.then_inc(bank_filled, 1)
                wait_bank(bank.x2t + 1)
                for n in range(NCH):
                    for r in range(4):
                        rows = slice(32 * r, 32 * r + 32)
                        mm = nc.tensor.matmul(g_ps[:, r, n * P:(n + 1) * P], x2t[rows, n, :],
                                              x0d[rows, q, n, :, :].rearrange("p a f -> p (a f)"), start=True, stop=True)
                mm.then_inc(gram_ps_done, 1)

            def layer3(t):
                for n in range(NP):
                    pe.wait_ge(w2_in[n % W2_RING], 16 * (NP // W2_RING * t + n // W2_RING + 1))
                    for e in range(W2_PIECE):
                        f = n * W2_PIECE + e
                        mm = nc.tensor.matmul(l1_ps[:, 0:BB], w2[:, n % W2_RING, e, :], gram[:, f, :],
                                              start=f == 0, stop=f == FIELDS - 1)
                    mm.then_inc(w2_used, 1)

            pe.wait_ge(ident_in, 16)
            pe.wait_ge(gathered, 16 * FIELDS)
            transpose_x0(0)
            for q in range(2):
                transpose_x0d(NX + q, q)
            pe.wait_ge(w0_folded, NI0 - 1)
            layer1(0)
            pe.wait_ge(w1_in, 16)

            def step(t, k, c):
                bank = TransposeBank(t, k, c)
                g0 = groups_before(c)
                layer2(g0, 0, k % 2)
                if bank.has_x0:
                    pe.wait_ge(gathered, 16 * FIELDS * (t + 2))
                    transpose_x0(bank.x0)
                if bank.has_x0d:
                    transpose_x0d(bank.x0d, (k + 2) % PER)
                g1 = g0 + NA
                if not is_step(c, NCB - 1):
                    pe.wait_ge(x1_ready, c + 1)
                    if k == 1:
                        pe.wait_ge(sum3_done, t + 1)
                    layer1(g1)
                    g1 = g1 + NB
                if k >= 1:
                    make_gram(c - 1, (k - 1) % PER, bank)
                layer2(g1, 1, k % 2)
                if k == PER:
                    pe.wait_ge(x1_ready, c + 2)
                    pe.wait_ge(gram_copied, 4 * c)
                    layer3(t)
                if k >= 1:
                    pe.wait_ge(x2_ready, c)

            walk(pe, step)
            make_gram(NCB - 1, PER - 1, TransposeBank(NBB, 0, NCB))
            pe.wait_ge(gram_copied, 4 * NCB)
            layer3(NBB - 1)

            pe.wait_ge(mlp_in, 16 * 7)
            pe.wait_ge(sum1_done, NCB)
            pe.wait_ge(sum2_done, NCB)
            pe.wait_ge(sum3_done, NBB + 1)
            for m in range(HID1 // P):
                for n in range(4):
                    rows = P if n < 3 else EMBED
                    rhs = sums[:, n, :] if n < 3 else dense[:, :]
                    mm = nc.tensor.matmul(g_ps[:, m, :], wt1[0:rows, n, m * P:(m + 1) * P], rhs, start=n == 0, stop=n == 3)
                mm.then_inc(mlp_ps_done, 1)
            for m in range(HID2 // P):
                for n in range(HID1 // P):
                    pe.wait_ge(mlp_ready, n + 1)
                    mm = nc.tensor.matmul(l2_ps[:, m, :], wt2[:, n, m * P:(m + 1) * P], hid1[:, n, :],
                                          start=n == 0, stop=n == HID1 // P - 1)
                mm.then_inc(mlp_ps_done, 1)
            for n in range(HID2 // P):
                pe.wait_ge(mlp_ready, HID1 // P + n + 1)
                mm = nc.tensor.matmul(t_ps[0:1, :], wt3[:, n:n + 1], hid2[:, n, :], start=n == 0, stop=n == HID2 // P - 1)
            mm.then_inc(mlp_ps_done, 1)


def kernel(**inputs):
    import numpy as np
    import concourse.bacc as bacc
    from concourse.bass_utils import run_bass_kernel_spmd

    a = {name: np.asarray(value) for name, value in inputs.items()}
    w0, w1, w2 = a["L0_rec_W0"], a["L0_rec_W1"], a["L0_rec_W2"]
    arrays = {
        "ids": a["ids"],
        "dense": a["dense_ctx"].T,
        "w0_hf": w0.reshape(MAPS, NI0, HT, NJ, FT).transpose(2, 4, 1, 3, 0).reshape(P, NI0, NJ, MAPS),
        "w0_fh": w0.reshape(MAPS, NJ, FT, NI0, HT).transpose(4, 2, 3, 1, 0).reshape(P, NI0, NJ, MAPS),
        "w1": w1.reshape(MAPS, NI1, HT, NJ, FT).transpose(2, 4, 1, 3, 0).reshape(P, NI1 * NJ, MAPS),
        "w2": w2.reshape(MAPS, MAPS, FIELDS).transpose(1, 2, 0),
        "cin_bias": np.stack([a["L0_rec_b0"], a["L0_rec_b1"], a["L0_rec_b2"]], axis=1),
        "wt1": a["W_top1"], "wt2": a["W_top2"],
        "wt3": a["W_top3"].reshape(HID2 // P, P).T,
        "bt1": a["b_top1"].reshape(HID1 // P, P).T,
        "bt2": a["b_top2"].reshape(HID2 // P, P).T,
        "ident": np.eye(P, dtype=np.float32),
        "pair_mask": (np.arange(P)[:, None] // EMBED % 2 == np.arange(2)).astype(np.float32),
    }
    arrays.update({f"tbl_{f}": a[f"tbl_{f}"] for f in range(FIELDS)})
    arrays = {name: np.ascontiguousarray(x) for name, x in arrays.items()}

    nc = bacc.Bacc("TRN2", target_bir_lowering=False, num_devices=1)
    aps = {name: nc.dram_tensor(f"in_{name}", x.shape, mybir.dt.from_np(x.dtype), kind="ExternalInput").ap()
           for name, x in arrays.items()}
    out = nc.dram_tensor("out", (BATCH, 1), F32, kind="ExternalOutput").ap()
    dlrm_tower(nc, aps, [aps[f"tbl_{f}"] for f in range(FIELDS)], out)
    r = run_bass_kernel_spmd(nc, [{f"in_{name}": x for name, x in arrays.items()}], core_ids=[0])
    return r.results[0]["out"]
```

```python
from contextlib import ExitStack

import concourse.bass as bass
from concourse import mybir

ALU = mybir.AluOpType
ACT = mybir.ActivationFunctionType
AX = mybir.AxisListType
F32 = mybir.dt.float32
I32 = mybir.dt.int32
U32 = mybir.dt.uint32
FR = mybir.dt.float32r

P = 128
BATCH, FIELDS, EMBED, MAPS = 512, 64, 16, 128
HID1, HID2 = 512, 256
BB = P
NBB = BATCH // BB
COLS = 512
CB = COLS // EMBED
PER = BB // CB
NCB = BATCH // CB
HT, FT = 16, 8
NI0, NI1, NJ = FIELDS // HT, MAPS // HT, FIELDS // FT
GROUP = 4
RING = 3
X1_RING = 4
W2_PIECE, W2_RING = 4, 4
NP = FIELDS // W2_PIECE
NCH = COLS // P
X0_DMAS = NJ + NI0
DPG = 4
NX = EMBED // DPG
HALF = P // 2

PAIR = "pair"
L1_GROUPS = [[(0, 0), (0, 2), (0, 4), (0, 6)], [(0, 3), (0, 5), (0, 7), (3, 6)],
             [(1, 2), (1, 4), (1, 6), (2, 7)], [(1, 5), (1, 7), (2, 4), (2, 6)],
             [(PAIR, 0), (PAIR, 2)]]
L1_SPLIT = [2, 1, 2, 1, 0]
L1_PRODUCTS = [[(0, 0, 0, 2, 4)], [(0, 0, 3, 2, 3), (3, 3, 6, 1, 1)], [(0, 1, 2, 2, 3), (3, 2, 7, 1, 1)],
               [(0, 1, 5, 2, 2), (2, 2, 4, 2, 2)], []]
L2_GROUPS = [[[(i, j + n) for n in range(GROUP)] for i in range(s * NI1 // 2, (s + 1) * NI1 // 2)
              for j in range(0, NJ, GROUP)] for s in range(2)]
L2_SPLIT = [2, 1] * (NI1 // 2)
FIRST, LAYER1, SECOND = range(3)
GROUPS = {FIRST: L2_GROUPS[0], LAYER1: L1_GROUPS, SECOND: L2_GROUPS[1]}
SPLIT = {FIRST: L2_SPLIT, LAYER1: L1_SPLIT, SECOND: L2_SPLIT}
PARTS = 3
NA, NB = len(L2_GROUPS[0]), len(L1_GROUPS)
NG = 2 * NA + NB
SB = sum(n > 0 for n in L1_SPLIT)
NS = 2 * NA + SB
assert NG * PER % RING == 0 and NI1 == 2 * X1_RING and SB % 2 == 0 and NA % 2 == 0 and NP % W2_RING == 0


def tiles_of(groups, split, whole):
    return [tile for group, n in zip(groups, split) for tile in (group[:len(group) - n] if whole else group[len(group) - n:])]


L1_WHOLE, L1_PARTS = (tiles_of(L1_GROUPS, L1_SPLIT, whole) for whole in (True, False))
L2_WHOLE, L2_PARTS = (tiles_of(L2_GROUPS[0] + L2_GROUPS[1], L2_SPLIT * 2, whole) for whole in (True, False))
NPARTS = len(L1_PARTS) + len(L2_PARTS)

STEP = [(FIRST, x) for x in range(NA)] + [(LAYER1, x) for x in range(NB)] + [(SECOND, x) for x in range(NA)]
LAST_STEP = [(place, x) for place, x in STEP if place != LAYER1]


def groups_before(c):
    return NG * c + NB


def splits_before(c):
    return NS * c + SB


def x0_copied(t):
    return NX if isinstance(t, int) and t == 0 else 12 * t + 2


class TransposeBank:

    def __init__(self, t, k, c):
        self.has_x0 = k == 2 and not isinstance(c, int)
        if k == 0:
            self.x2t = 12 * NBB - 1
            self.x0d = NX + 1
        else:
            self.x2t = 12 * t + (0, 6, 8, 14, 16)[k] - (4 if isinstance(c, int) and k == 3 else 0)
            self.x0d = self.x2t + 1
        self.x0 = self.x0d + 1


def repeat_each(rows, n):
    (step, r), (cs, cols) = rows.ap
    return bass.AP(rows.tensor, rows.offset, [[step, r], [0, n], [cs, cols]])


def repeat_set(rows, n):
    (step, r), (cs, cols) = rows.ap
    return bass.AP(rows.tensor, rows.offset, [[0, n], [step, r], [cs, cols]])


def dlrm_tower(nc, ins, tables, out):
    with ExitStack() as ctx:
        def sb(name, shape, dt=F32):
            return ctx.enter_context(nc.sbuf_tensor(name, shape, dt))

        def ps(name, shape):
            return ctx.enter_context(nc.psum_tensor(name, shape, F32))

        def sem(name):
            return ctx.enter_context(nc.semaphore(name))

        w0 = sb("w0", [P, len(L1_WHOLE), P])
        w1 = sb("w1", [P, len(L2_WHOLE), P])
        w_high = sb("w_high", [P, NPARTS, P], FR)
        w_low = sb("w_low", [P, NPARTS, P], FR)
        w2 = sb("w2", [P, W2_RING, W2_PIECE, P])
        wt3 = sb("wt3", [P, HID2 // P])
        cin_bias = sb("cin_bias", [P, 3])
        bias3_sum = sb("bias3_sum", [P, 1])
        bt1 = sb("bt1", [P, HID1 // P])
        bt2 = sb("bt2", [P, HID2 // P])
        ident = sb("ident", [P, P])
        pair_mask = sb("pair_mask", [P, 2])
        ids = sb("ids", [P, NBB, FIELDS], I32)
        emb = sb("emb", [P, FIELDS, EMBED])
        x0 = sb("x0", [P, HALF, EMBED])
        x0f = sb("x0f", [P, 2, NJ, COLS])
        x0h = sb("x0h", [P, NI0, COLS])
        x1 = sb("x1", [P, COLS])
        x1h = sb("x1h", [P, X1_RING, COLS])
        prod = sb("prod", [P, RING, GROUP, COLS])
        high = sb("high", [P, PARTS, COLS], FR)
        low = sb("low", [P, PARTS, COLS], FR)
        x2 = sb("x2", [P, COLS])
        x2t = sb("x2t", [P, NCH, MAPS])
        x0d = sb("x0d", [P, 2, NCH, 2, FIELDS])
        gram = sb("gram", [P, FIELDS, BB])
        sums = sb("sums", [P, 3, BATCH])
        staged = gram[:, :, :].rearrange("p f b -> p (f b)")
        parts_raw = staged[:, 0:NPARTS * P].rearrange("p (n o) -> p n o", o=P)
        n_second = len(L1_WHOLE) + len(L1_PARTS) - 2
        w0_second = staged[:, NPARTS * P:(NPARTS + n_second) * P].rearrange("p (n o) -> p n o", o=P)
        wt1 = x0f[:, 1, 0:4, :]
        wt2 = x0f[:, 1, 4:6, :].rearrange("p a n -> p (a n)").rearrange("p (k n) -> p k n", n=HID2)
        dense = x0f[0:EMBED, 1, 6, :]
        hid1 = x0f[:, 0, 0:4, :]
        hid2 = x0f[:, 0, 4:6, :]
        y = x0f[:, 0, 6, :]
        x0_dram = nc.dram_tensor("x0_dram", (NBB, FIELDS, BB * EMBED), F32, kind="Internal").ap()

        l1_ps = ps("l1_ps", [P, COLS])
        l2_ps = ps("l2_ps", [P, 2, COLS])
        t_ps = ps("t_ps", [P, COLS])
        g_ps = ps("g_ps", [P, 4, COLS])

        ids_in, ident_in, mask_in, bias_in = sem("ids_in"), sem("ident_in"), sem("mask_in"), sem("bias_in")
        w0_in, w1_in, parts_in, mlp_in = sem("w0_in"), sem("w1_in"), sem("parts_in"), sem("mlp_in")
        w0_folded, w_high_ready, w_low_ready = sem("w0_folded"), sem("w_high_ready"), sem("w_low_ready")
        gathered = sem("gathered")
        bank_filled, bank_copied = sem("bank_filled"), sem("bank_copied")
        x0_stored, x0_in = sem("x0_stored"), sem("x0_in")
        x1h_in = [sem(f"x1h_in{r}") for r in range(X1_RING)]
        prod_ready, prod_used = sem("prod_ready"), sem("prod_used")
        high_ready, low_ready, split_used = sem("high_ready"), sem("low_ready"), sem("split_used")
        x1_ready, x2_ready = sem("x1_ready"), sem("x2_ready")
        sum1_done, sum2_done = sem("sum1_done"), sem("sum2_done")
        sum3_done = sem("sum3_done")
        gram_ps_done, gram_copied = sem("gram_ps_done"), sem("gram_copied")
        w2_in = [sem(f"w2_in{r}") for r in range(W2_RING)]
        w2_used = sem("w2_used")
        mlp_ps_done, mlp_ready = sem("mlp_ps_done"), sem("mlp_ready")
        out_written = sem("out_written")

        def walk(eng, step):
            step(0, 0, 0)
            with eng.Fori(0, NBB - 1) as t:
                for k in range(1, PER + 1):
                    step(t, k, t * PER + k)
            for k in range(1, PER):
                step(NBB - 1, k, PER * (NBB - 1) + k)

        def is_last(c):
            return isinstance(c, int) and c == NCB - 1

        def groups(k, c):
            split = 0
            for n, (place, x) in enumerate(LAST_STEP if is_last(c) else STEP):
                yield n, place, x, (NB + NG * k + n) % RING, split
                split += SPLIT[place][x] > 0

        def part_slots(split, count):
            return slice(0, 2) if count == 2 else slice(2, 3)

        block = ctx.enter_context(nc.Block())

        @block.gpsimd
        def _(pool):
            pool.wait_ge(ids_in, 16)
            for t in range(NBB):
                if t:
                    pool.wait_ge(bank_copied, x0_copied(t - 1))
                for f in range(FIELDS):
                    nc.gpsimd.indirect_dma_start(
                        out=emb[:, f, :], out_offset=None, in_=tables[f],
                        in_offset=bass.IndirectOffsetOnAxis(ap=ids[:, t, f:f + 1].bitcast(U32), axis=0),
                    ).then_inc(gathered, 16)
                pool.wait_ge(gathered, 16 * FIELDS * (t + 1))

        @block.sync
        def _(sp):
            sp.dma_start(ids[:, :, :], ins["ids"].rearrange("(t p) f -> p t f", p=P)).then_inc(ids_in, 16)
            sp.dma_start(ident[:, :], ins["ident"]).then_inc(ident_in, 16)
            sp.dma_start(w0[:, :, :], ins["w0_first"][:, 0:len(L1_WHOLE), :]).then_inc(w0_in, 16)
            sp.dma_start(parts_raw[:, 0:len(L1_PARTS), :], ins["w0_first"][:, len(L1_WHOLE):, :]).then_inc(w0_in, 16)
            sp.dma_start(w0_second, ins["w0_second"]).then_inc(w0_in, 16)
            sp.dma_start(cin_bias[:, :], ins["cin_bias"]).then_inc(bias_in, 16)
            sp.dma_start(parts_raw[:, len(L1_PARTS):, :], ins["w1_parts"]).then_inc(parts_in, 16)
            sp.dma_start(w1[:, :, :], ins["w1_whole"]).then_inc(w1_in, 16)
            sp.dma_start(pair_mask[:, :], ins["pair_mask"]).then_inc(mask_in, 16)

            def store_x0(t):
                for half in range(2):
                    sp.dma_start(x0_dram[t, :, half * HALF * EMBED:(half + 1) * HALF * EMBED],
                                 x0[half * HALF:(half + 1) * HALF, :, :].rearrange("f b d -> f (b d)")).then_inc(x0_stored, 16)

            def load_x0(t, q, b):
                rows = x0_dram[t, :, q * COLS:(q + 1) * COLS]
                for i in range(NI0):
                    sp.dma_start(x0h[:, i, :], repeat_each(rows[HT * i:HT * (i + 1), :], FT)).then_inc(x0_in, 16)
                for j in range(NJ):
                    sp.dma_start(x0f[:, b, j, :], repeat_set(rows[FT * j:FT * (j + 1), :], HT)).then_inc(x0_in, 16)

            def load_x1(i):
                sp.dma_start(x1h[:, i % X1_RING, :],
                             repeat_each(x1[HT * i:HT * (i + 1), :], FT)).then_inc(x1h_in[i % X1_RING], 16)

            def load_w2(n):
                sp.dma_start(w2[:, n % W2_RING, :, :],
                             ins["w2"][:, n * W2_PIECE:(n + 1) * W2_PIECE, :]).then_inc(w2_in[n % W2_RING], 16)

            sp.wait_ge(bank_copied, x0_copied(0))
            store_x0(0)
            sp.wait_ge(x0_stored, 32)
            load_x0(0, 0, 0)
            for n in range(W2_RING):
                load_w2(n)
            sp.wait_ge(x1_ready, 1)
            for i in range(X1_RING):
                load_x1(i)

            def step(t, k, c):
                if not is_last(c):
                    if k == PER - 1:
                        sp.wait_ge(x0_stored, 32 * (t + 2))
                    elif k == 0:
                        sp.wait_ge(prod_ready, NB)
                    load_x0(t + (k + 1) // PER, (k + 1) % PER, (k + 1) % 2)
                for i in range(X1_RING):
                    sp.wait_ge(prod_ready, groups_before(c) + 2 * i + 2)
                    load_x1(X1_RING + i)
                if is_last(c):
                    return
                sp.wait_ge(sum1_done, c + 2)
                load_x1(0)
                load_x1(1)
                for i in range(2, X1_RING):
                    sp.wait_ge(prod_ready, groups_before(c) + NA + NB + 2 * i + 2)
                    load_x1(i)
                if TransposeBank(t, k, c).has_x0:
                    sp.wait_ge(bank_copied, x0_copied(t + 1))
                    store_x0(t + 1)
                if k == PER:
                    for n in range(NP):
                        sp.wait_ge(w2_used, t * NP + n + 1)
                        load_w2((n + W2_RING) % NP)

            walk(sp, step)
            sp.wait_ge(prod_ready, groups_before(NCB) - NB)
            sp.dma_start(wt1[:, 0:3, :], ins["wt1"][0:3 * P, :].rearrange("(k p) n -> p k n", p=P)).then_inc(mlp_in, 16)
            sp.dma_start(wt1[0:EMBED, 3, :], ins["wt1"][3 * P:3 * P + EMBED, :]).then_inc(mlp_in, 16)
            sp.dma_start(wt2, ins["wt2"].rearrange("(k p) n -> p k n", p=P)).then_inc(mlp_in, 16)
            sp.dma_start(dense, ins["dense"]).then_inc(mlp_in, 16)
            sp.dma_start(wt3[:, :], ins["wt3"]).then_inc(mlp_in, 16)
            sp.dma_start(bt1[:, :], ins["bt1"]).then_inc(mlp_in, 16)
            sp.dma_start(bt2[:, :], ins["bt2"]).then_inc(mlp_in, 16)
            for n in range(NP - W2_RING):
                sp.wait_ge(w2_used, (NBB - 1) * NP + n + 1)
                load_w2(n + W2_RING)
            sp.wait_ge(mlp_ready, 7)
            sp.dma_start(out.rearrange("b a -> a b"), y[0:1, :]).then_inc(out_written, 16)
            sp.wait_ge(out_written, 16)

        @block.vector
        def _(dve):
            dve.wait_ge(w0_in, 16 * 3)
            n = 0
            for home, tiles in ((w0, L1_WHOLE), (parts_raw, L1_PARTS)):
                for at, (i, j) in enumerate(tiles):
                    if i == PAIR:
                        continue
                    rows = slice(HALF if j == 2 * i else 0, P)
                    nc.vector.tensor_tensor(home[rows, at, :], home[rows, at, :], w0_second[rows, n, :],
                                            ALU.add).then_inc(w0_folded, 1)
                    n += 1
            for s, (a, b) in enumerate(((0, len(L1_PARTS)), (len(L1_PARTS), NPARTS))):
                dve.wait_ge(w_high_ready, s + 1)
                nc.vector.tensor_tensor(w_low[:, a:b, :], parts_raw[:, a:b, :], w_high[:, a:b, :].bitcast(F32),
                                        ALU.subtract).then_inc(w_low_ready, 1)

            def product(place, x, g, lows, buf, b):
                if not (isinstance(g, int) and g < RING):
                    dve.wait_ge(prod_used, g - (RING - 1))
                    dve.wait_ge(low_ready, lows)
                if place == LAYER1:
                    parts = [(prod[:, buf, s:s + n, :], x0h[:, i, :].unsqueeze(1).to_broadcast([P, n, COLS]),
                              x0f[:, b, j:j + (n - 1) * step + 1:step, :]) for s, i, j, step, n in L1_PRODUCTS[x]]
                    for s, (kind, i) in enumerate(L1_GROUPS[x]):
                        if kind == PAIR:
                            for rows, e in ((slice(HALF, P), i), (slice(0, HALF), i + 1)):
                                parts.append((prod[rows, buf, s, :], x0h[HALF:P, e, :], x0f[HALF:P, b, 2 * e + 1, :]))
                else:
                    i, j = GROUPS[place][x][0]
                    parts = [(prod[:, buf, :, :], x1h[:, i % X1_RING, :].unsqueeze(1).to_broadcast([P, GROUP, COLS]),
                              x0f[:, b, j:j + GROUP, :])]
                for to, left, right in parts:
                    ins_ = nc.vector.tensor_tensor(to, left, right, ALU.mult)
                ins_.then_inc(prod_ready, 1)

            def low_part(place, x, split, buf):
                count = SPLIT[place][x]
                slots = part_slots(split, count)
                dve.wait_ge(high_ready, split + 1)
                nc.vector.tensor_tensor(low[:, slots, :], prod[:, buf, len(GROUPS[place][x]) - count:len(GROUPS[place][x]), :],
                                        high[:, slots, :].bitcast(F32), ALU.subtract).then_inc(low_ready, 1)

            def x0_diagonal(index, b):
                dve.wait_ge(bank_filled, index + 1)
                nc.vector.tensor_tensor(
                    x0d[:, b, :, :, :],
                    t_ps[:, 0:NCH * FIELDS].rearrange("p (n f) -> p n f", f=FIELDS).unsqueeze(2).to_broadcast(
                        [P, NCH, 2, FIELDS]),
                    pair_mask[:, :].unsqueeze(1).unsqueeze(3).to_broadcast([P, NCH, 2, FIELDS]),
                    ALU.mult).then_inc(bank_copied, 1)

            def sum_dims(x, layer, c, done):
                nc.vector.tensor_reduce(sums[:, layer, bass.ds(c * CB, CB)],
                                        x[:, :].rearrange("p (b d) -> p b d", d=EMBED), AX.X, ALU.add).then_inc(done, 1)

            dve.wait_ge(mask_in, 16)
            x0_diagonal(NX, 0)
            dve.wait_ge(x0_in, 16 * X0_DMAS)
            split = 0
            for x in range(NB):
                product(LAYER1, x, x, x - RING + 1, x % RING, 0)
                if x:
                    low_part(LAYER1, x - 1, split, (x - 1) % RING)
                    split += 1
            dve.wait_ge(x1_ready, 1)
            sum_dims(x1, 0, 0, sum1_done)

            def step(t, k, c):
                bank = TransposeBank(t, k, c)
                g0, s0 = groups_before(c), splits_before(c)
                earlier = []
                for n, place, x, buf, split in groups(k, c):
                    if place != LAYER1 and x % 2 == 0:
                        dve.wait_ge(x1h_in[x // 2], 16 * (2 * c + (1 if place == FIRST else 2)))
                    if (place, x) == (LAYER1, 0):
                        dve.wait_ge(x0_in, 16 * X0_DMAS * (c + 2))
                    if n >= RING:
                        lows = s0 + earlier[n - RING]
                    elif k:
                        lows = s0 - (RING - 1) + n
                    else:
                        lows = min(SB, NB - RING + 1 + n)
                    product(place, x, g0 + n, lows, buf, (k + 1) % 2 if place == LAYER1 else k % 2)
                    if n == 0:
                        if k:
                            low_part(SECOND, NA - 1, s0 - 1, (NB + NG * k - 1) % RING)
                    elif SPLIT[last[0]][last[1]]:
                        low_part(last[0], last[1], s0 + last[3], last[2])
                    last = (place, x, buf, split)
                    earlier.append(split + (SPLIT[place][x] > 0))
                    if k and (place, x) == (FIRST, 5):
                        dve.wait_ge(x2_ready, c)
                        sum_dims(x2, 1, c - 1, sum2_done)
                    if not is_last(c) and (place, x) == (SECOND, 2):
                        x0_diagonal(bank.x0d, (k + 1) % 2)
                    if not is_last(c) and (place, x) == (SECOND, 3):
                        dve.wait_ge(x1_ready, c + 2)
                        sum_dims(x1, 0, c + 1, sum1_done)

            walk(dve, step)
            g_last = groups_before(NCB) - NB - 1
            low_part(SECOND, NA - 1, splits_before(NCB) - SB - 1, g_last % RING)
            dve.wait_ge(x2_ready, NCB)
            sum_dims(x2, 1, NCB - 1, sum2_done)

        @block.scalar
        def _(act):
            act.wait_ge(w0_folded, n_second)
            nc.scalar.activation(w_high[:, 0:len(L1_PARTS), :], parts_raw[:, 0:len(L1_PARTS), :],
                                 ACT.Copy).then_inc(w_high_ready, 1)
            act.wait_ge(parts_in, 16)
            nc.scalar.activation(w_high[:, len(L1_PARTS):, :], parts_raw[:, len(L1_PARTS):, :],
                                 ACT.Copy).then_inc(w_high_ready, 1)
            act.wait_ge(bias_in, 16)
            nc.scalar.mul(bias3_sum[:, :], cin_bias[:, 2:3], float(EMBED)).then_inc(sum3_done, 1)

            def high_part(place, x, g, split, buf):
                count = SPLIT[place][x]
                slots = part_slots(split, count)
                if not (isinstance(split, int) and split < 2):
                    act.wait_ge(split_used, split - 1)
                act.wait_ge(prod_ready, g + 1)
                nc.scalar.activation(high[:, slots, :],
                                     prod[:, buf, len(GROUPS[place][x]) - count:len(GROUPS[place][x]), :],
                                     ACT.Copy).then_inc(high_ready, 1)

            def copy_x0(index, n):
                act.wait_ge(bank_filled, index + n + 1)
                for half in range(2):
                    ins_ = nc.scalar.activation(
                        x0[half * HALF:(half + 1) * HALF, :, n * DPG:(n + 1) * DPG].rearrange("f b d -> f d b"),
                        t_ps[0:FIELDS, :].rearrange("f (d b) -> f d b", d=DPG)[:, :, half * HALF:(half + 1) * HALF],
                        ACT.Copy)
                ins_.then_inc(bank_copied, 1)

            def store_x1(used):
                act.wait_ge(prod_used, used)
                nc.scalar.activation(x1[:, :], l1_ps[:, :], ACT.Identity, bias=cin_bias[:, 0:1]).then_inc(x1_ready, 1)

            def store_x2(c, b):
                act.wait_ge(split_used, splits_before(c) + NS - SB * is_last(c))
                nc.scalar.activation(x2[:, :], l2_ps[:, b, :], ACT.Identity,
                                     bias=cin_bias[:, 1:2]).then_inc(x2_ready, 1)

            def store_x2t(bank):
                act.wait_ge(bank_filled, bank.x2t + 1)
                nc.scalar.activation(x2t[:, :, :].rearrange("p n h -> p (n h)"), t_ps[:, :],
                                     ACT.Copy).then_inc(bank_copied, 1)

            def store_gram(c, q, r):
                if r == 0:
                    act.wait_ge(gram_ps_done, c + 1)
                to = gram[:, :, q * CB:(q + 1) * CB].rearrange("h f (n r a) -> h r n a f", n=NCH, r=4)[:, r]
                nc.scalar.activation(to, g_ps[:, r, :].rearrange("h (n a f) -> h n a f", n=NCH, a=2),
                                     ACT.Copy).then_inc(gram_copied, 1)

            def store_sum3(t):
                act.wait_ge(sum3_done, t + 1)
                act.wait_ge(w2_used, NP * t + NP)
                nc.scalar.activation(sums[:, 2, bass.ds(t * BB, BB)], l1_ps[:, 0:BB], ACT.Identity,
                                     bias=bias3_sum[:, 0:1]).then_inc(sum3_done, 1)

            for n in range(NX):
                copy_x0(0, n)
            for x in range(SB):
                high_part(LAYER1, x, x, x, x % RING)
            store_x1(NB)

            def step(t, k, c):
                bank = TransposeBank(t, k, c)
                g0, s0 = groups_before(c), splits_before(c)
                if bank.has_x0:
                    act.wait_ge(x0_stored, 32 * (t + 1))
                for n, place, x, buf, split in groups(k, c):
                    if SPLIT[place][x]:
                        high_part(place, x, g0 + n, s0 + split, buf)
                    if k and (place, x) == (FIRST, 0):
                        store_x2(c - 1, (k - 1) % 2)
                    if k and (place, x) == ((SECOND, 0) if is_last(c) else (LAYER1, 0)):
                        store_x2t(bank)
                    if not is_last(c) and (place, x) == (SECOND, 0):
                        for r in range(X1_RING):
                            act.wait_ge(x1h_in[r], 16 * (2 * c + 2))
                        act.wait_ge(sum1_done, c + 1)
                        store_x1(g0 + NA + NB)
                    if k and place == SECOND and 1 <= x <= 4:
                        store_gram(c - 1, (k - 1) % PER, x - 1)
                    if bank.has_x0 and place == SECOND and x in (4, 5, 6, 7):
                        copy_x0(bank.x0, x - 4)
                if k == PER:
                    store_sum3(t)

            walk(act, step)
            store_x2(NCB - 1, (NCB - 1) % 2)
            store_x2t(TransposeBank(NBB, 0, NCB))
            for r in range(4):
                store_gram(NCB - 1, PER - 1, r)
            store_sum3(NBB - 1)
            act.wait_ge(mlp_in, 16 * 7)
            for m in range(HID1 // P):
                act.wait_ge(mlp_ps_done, m + 1)
                nc.scalar.activation(hid1[:, m, :], g_ps[:, m, :], ACT.Relu, bias=bt1[:, m:m + 1]).then_inc(mlp_ready, 1)
            for m in range(HID2 // P):
                act.wait_ge(mlp_ps_done, HID1 // P + m + 1)
                nc.scalar.activation(hid2[:, m, :], l2_ps[:, m, :], ACT.Relu, bias=bt2[:, m:m + 1]).then_inc(mlp_ready, 1)
            act.wait_ge(mlp_ps_done, HID1 // P + HID2 // P + 1)
            nc.scalar.activation(y[0:1, :], t_ps[0:1, :], ACT.Copy).then_inc(mlp_ready, 1)

        @block.tensor
        def _(pe):
            def wait_bank(n):
                if not (isinstance(n, int) and n == 0):
                    pe.wait_ge(bank_copied, n)

            def turn(to, rows, n):
                a, m = rows.base_partition(), rows.partition_size()
                unit = ident[a:a + m, a:a + m]
                if n == 0:
                    return nc.tensor.matmul(to, rows, unit, start=True, stop=True)
                return nc.tensor.transpose(to, rows, unit)

            def transpose_x0(index, n):
                wait_bank(index + n)
                for e in range(DPG):
                    mm = turn(t_ps[0:FIELDS, e * BB:(e + 1) * BB], emb[:, :, n * DPG + e], e)
                mm.then_inc(bank_filled, 1)

            def transpose_x0d(index, q):
                wait_bank(index)
                half, at = divmod(q * CB, HALF)
                rows = x0[half * HALF:(half + 1) * HALF, at:at + CB, :].rearrange("f b d -> f (b d)")
                for n in range(NCH):
                    mm = turn(t_ps[:, n * FIELDS:(n + 1) * FIELDS], rows[:, n * P:(n + 1) * P], n)
                mm.then_inc(bank_filled, 1)

            def contract(place, x, g, split, buf, acc, whole, whole_at, parts_at):
                tiles, count = len(GROUPS[place][x]), SPLIT[place][x]
                start = (place, x) in ((FIRST, 0), (LAYER1, 0))
                stop = (place, x) in ((SECOND, NA - 1), (LAYER1, NB - 1))
                pe.wait_ge(prod_ready, g + 1)
                for n in range(tiles - count):
                    mm = nc.tensor.matmul(acc, whole[:, whole_at + n, :], prod[:, buf, n, :], start=start and n == 0,
                                          stop=stop and not count and n == tiles - 1)
                mm.then_inc(prod_used, 1)
                if not count:
                    return
                pe.wait_ge(low_ready, split + 1)
                slots = part_slots(split, count)
                for n in range(count):
                    at, s = parts_at + n, slots.start + n
                    nc.tensor.matmul(acc, w_high[:, at, :], high[:, s, :], start=False, stop=False)
                    nc.tensor.matmul(acc, w_high[:, at, :], low[:, s, :], start=False, stop=False)
                    mm = nc.tensor.matmul(acc, w_low[:, at, :], high[:, s, :], start=False,
                                          stop=stop and n == count - 1)
                mm.then_inc(split_used, 1)

            def weights_at(place, x):
                if place == LAYER1:
                    split = sum(L1_SPLIT[:x])
                    return sum(len(g) for g in L1_GROUPS[:x]) - split, split
                split = sum(L2_SPLIT[:x]) + (sum(L2_SPLIT) if place == SECOND else 0)
                return GROUP * (x + NA * (place == SECOND)) - split, len(L1_PARTS) + split

            def transpose_x2(c, bank):
                pe.wait_ge(x2_ready, c + 1)
                wait_bank(bank.x2t)
                for n in range(NCH):
                    mm = nc.tensor.transpose(t_ps[:, n * P:(n + 1) * P], x2[:, n * P:(n + 1) * P], ident[:, :])
                mm.then_inc(bank_filled, 1)

            def make_gram(b, bank):
                wait_bank(bank.x2t + 1)
                for n in range(NCH):
                    for r in range(4):
                        rows = slice(32 * r, 32 * r + 32)
                        mm = nc.tensor.matmul(g_ps[:, r, n * P:(n + 1) * P], x2t[rows, n, :],
                                              x0d[rows, b, n, :, :].rearrange("p a f -> p (a f)"), start=True, stop=True)
                mm.then_inc(gram_ps_done, 1)

            def layer3(t):
                for n in range(NP):
                    pe.wait_ge(w2_in[n % W2_RING], 16 * (NP // W2_RING * t + n // W2_RING + 1))
                    for e in range(W2_PIECE):
                        f = n * W2_PIECE + e
                        mm = nc.tensor.matmul(l1_ps[:, 0:BB], w2[:, n % W2_RING, e, :], gram[:, f, :],
                                              start=f == 0, stop=f == FIELDS - 1)
                    mm.then_inc(w2_used, 1)

            pe.wait_ge(ident_in, 16)
            pe.wait_ge(gathered, 16 * FIELDS)
            for n in range(NX):
                transpose_x0(0, n)
            transpose_x0d(NX, 0)
            pe.wait_ge(w_low_ready, 1)
            split = 0
            for x in range(NB):
                contract(LAYER1, x, x, split, x % RING, l1_ps[:, :], w0, *weights_at(LAYER1, x))
                split += L1_SPLIT[x] > 0
            pe.wait_ge(w1_in, 16)
            pe.wait_ge(w_low_ready, 2)

            def step(t, k, c):
                bank = TransposeBank(t, k, c)
                g0, s0 = groups_before(c), splits_before(c)
                for n, place, x, buf, split in groups(k, c):
                    if (place, x) == (LAYER1, 0):
                        pe.wait_ge(x1_ready, c + 1)
                        if k == 1:
                            pe.wait_ge(sum3_done, t + 1)
                    if place == LAYER1:
                        contract(place, x, g0 + n, s0 + split, buf, l1_ps[:, :], w0, *weights_at(place, x))
                    else:
                        contract(place, x, g0 + n, s0 + split, buf, l2_ps[:, k % 2, :], w1, *weights_at(place, x))
                    if k and (place, x) == (FIRST, NA - 1):
                        transpose_x2(c - 1, bank)
                    if (place, x) == (FIRST if is_last(c) else LAYER1, NA - 1 if is_last(c) else NB - 1):
                        if k:
                            make_gram((k - 1) % 2, bank)
                        if not is_last(c):
                            transpose_x0d(bank.x0d, (k + 1) % PER)
                    if bank.has_x0 and place == SECOND and x in (2, 3, 4, 5):
                        if x == 2:
                            pe.wait_ge(gathered, 16 * FIELDS * (t + 2))
                        transpose_x0(bank.x0, x - 2)
                if k == PER:
                    pe.wait_ge(x1_ready, c + 2)
                    pe.wait_ge(gram_copied, 4 * c)
                    layer3(t)
                if k >= 1:
                    pe.wait_ge(x2_ready, c)

            walk(pe, step)
            bank = TransposeBank(NBB, 0, NCB)
            transpose_x2(NCB - 1, bank)
            make_gram((NCB - 1) % 2, bank)
            pe.wait_ge(gram_copied, 4 * NCB)
            layer3(NBB - 1)

            pe.wait_ge(mlp_in, 16 * 7)
            pe.wait_ge(sum1_done, NCB)
            pe.wait_ge(sum2_done, NCB)
            pe.wait_ge(sum3_done, NBB + 1)
            for m in range(HID1 // P):
                for n in range(4):
                    rows = P if n < 3 else EMBED
                    rhs = sums[:, n, :] if n < 3 else dense
                    mm = nc.tensor.matmul(g_ps[:, m, :], wt1[0:rows, n, m * P:(m + 1) * P], rhs, start=n == 0, stop=n == 3)
                mm.then_inc(mlp_ps_done, 1)
            for m in range(HID2 // P):
                for n in range(HID1 // P):
                    pe.wait_ge(mlp_ready, n + 1)
                    mm = nc.tensor.matmul(l2_ps[:, m, :], wt2[:, n, m * P:(m + 1) * P], hid1[:, n, :],
                                          start=n == 0, stop=n == HID1 // P - 1)
                mm.then_inc(mlp_ps_done, 1)
            for n in range(HID2 // P):
                pe.wait_ge(mlp_ready, HID1 // P + n + 1)
                mm = nc.tensor.matmul(t_ps[0:1, :], wt3[:, n:n + 1], hid2[:, n, :], start=n == 0, stop=n == HID2 // P - 1)
            mm.then_inc(mlp_ps_done, 1)


def kernel(**inputs):
    import numpy as np
    import concourse.bacc as bacc
    from concourse.bass_utils import run_bass_kernel_spmd

    a = {name: np.asarray(value) for name, value in inputs.items()}
    w0, w1, w2 = a["L0_rec_W0"], a["L0_rec_W1"], a["L0_rec_W2"]
    w0_hf = w0.reshape(MAPS, NI0, HT, NJ, FT).transpose(1, 3, 2, 4, 0).reshape(NI0, NJ, P, MAPS)
    w0_fh = w0.reshape(MAPS, NJ, FT, NI0, HT).transpose(3, 1, 4, 2, 0).reshape(NI0, NJ, P, MAPS)
    w1_hf = w1.reshape(MAPS, NI1, HT, NJ, FT).transpose(1, 3, 2, 4, 0).reshape(NI1, NJ, P, MAPS)

    def w0_tile(i, j):
        if i == PAIR:
            return np.concatenate([w0_hf[j + 1, 2 * j + 3, HALF:], w0_hf[j, 2 * j + 1, HALF:]])
        return w0_hf[i, j]

    l1_tiles = L1_WHOLE + L1_PARTS
    arrays = {
        "ids": a["ids"],
        "dense": a["dense_ctx"].T,
        "w0_first": np.stack([w0_tile(i, j) for i, j in l1_tiles], axis=1),
        "w0_second": np.stack([w0_fh[i, j] for i, j in l1_tiles if i != PAIR], axis=1),
        "w1_whole": np.stack([w1_hf[i, j] for i, j in L2_WHOLE], axis=1),
        "w1_parts": np.stack([w1_hf[i, j] for i, j in L2_PARTS], axis=1),
        "w2": w2.reshape(MAPS, MAPS, FIELDS).transpose(1, 2, 0),
        "cin_bias": np.stack([a["L0_rec_b0"], a["L0_rec_b1"], a["L0_rec_b2"]], axis=1),
        "wt1": a["W_top1"], "wt2": a["W_top2"],
        "wt3": a["W_top3"].reshape(HID2 // P, P).T,
        "bt1": a["b_top1"].reshape(HID1 // P, P).T,
        "bt2": a["b_top2"].reshape(HID2 // P, P).T,
        "ident": np.eye(P, dtype=np.float32),
        "pair_mask": (np.arange(P)[:, None] // EMBED % 2 == np.arange(2)).astype(np.float32),
    }
    arrays.update({f"tbl_{f}": a[f"tbl_{f}"] for f in range(FIELDS)})
    arrays = {name: np.ascontiguousarray(x) for name, x in arrays.items()}

    nc = bacc.Bacc("TRN2", target_bir_lowering=False, num_devices=1)
    aps = {name: nc.dram_tensor(f"in_{name}", x.shape, mybir.dt.from_np(x.dtype), kind="ExternalInput").ap()
           for name, x in arrays.items()}
    out = nc.dram_tensor("out", (BATCH, 1), F32, kind="ExternalOutput").ap()
    dlrm_tower(nc, aps, [aps[f"tbl_{f}"] for f in range(FIELDS)], out)
    r = run_bass_kernel_spmd(nc, [{f"in_{name}": x for name, x in arrays.items()}], core_ids=[0])
    return r.results[0]["out"]
```

```python
from contextlib import ExitStack

import concourse.bass as bass
from concourse import mybir

ALU = mybir.AluOpType
ACT = mybir.ActivationFunctionType
AX = mybir.AxisListType
F32 = mybir.dt.float32
I32 = mybir.dt.int32
U32 = mybir.dt.uint32
FR = mybir.dt.float32r

P = 128
BATCH, FIELDS, EMBED, MAPS = 512, 64, 16, 128
HID1, HID2 = 512, 256
BB = P
NBB = BATCH // BB
COLS = 512
CB = COLS // EMBED
PER = BB // CB
NCB = BATCH // CB
HT, FT = 16, 8
NI0, NI1, NJ = FIELDS // HT, MAPS // HT, FIELDS // FT
GROUP = 4
RING = 3
X1_RING = 4
W2_PIECE, W2_RING = 4, 4
NP = FIELDS // W2_PIECE
NCH = COLS // P
X0_DMAS = NJ + NI0
GF = P // CB
NGA = FIELDS // GF
HALF = P // 2

PAIR = "pair"
L1_GROUPS = [[(0, 0), (0, 2), (0, 4), (0, 6)], [(0, 3), (0, 5), (0, 7), (3, 6)],
             [(1, 2), (1, 4), (1, 6), (2, 7)], [(1, 5), (1, 7), (2, 4), (2, 6)],
             [(PAIR, 0), (PAIR, 2)]]
L1_SPLIT = [2, 1, 2, 1, 0]
L1_PRODUCTS = [[(0, 0, 0, 2, 4)], [(0, 0, 3, 2, 3), (3, 3, 6, 1, 1)], [(0, 1, 2, 2, 3), (3, 2, 7, 1, 1)],
               [(0, 1, 5, 2, 2), (2, 2, 4, 2, 2)], []]
L2_GROUPS = [[[(i, j + n) for n in range(GROUP)] for i in range(s * NI1 // 2, (s + 1) * NI1 // 2)
              for j in range(0, NJ, GROUP)] for s in range(2)]
L2_SPLIT = [1, 2, 2, 2] * (NI1 // 4)
START_GROUPS = [[(0, 0)], [(0, 2), (0, 3), (1, 2), (PAIR, 0)], [(0, 5), (1, 4), (1, 5), (2, 4)],
                [(0, 7), (0, 4), (0, 6)], [(3, 6)], [(1, 6), (2, 7)], [(2, 6)], [(1, 7), (PAIR, 2)]]
START_SPLIT = [0, 0, 0, 2, 1, 2, 1, 0]
START_QUARTER = [0, 1, 2, 3, 3, 3, 3, 3]
START_PRODUCTS = [[(0, 0, 0, 1, 1)], [(0, 0, 2, 1, 2), (2, 1, 2, 1, 1)], [(0, 0, 5, 1, 1), (1, 1, 4, 1, 2), (3, 2, 4, 1, 1)],
                  [(0, 0, 7, 1, 1), (1, 0, 4, 2, 2)], [(0, 3, 6, 1, 1)], [(0, 1, 6, 1, 1), (1, 2, 7, 1, 1)],
                  [(0, 2, 6, 1, 1)], [(0, 1, 7, 1, 1)]]
QG = NGA // 4
FIRST, LAYER1, SECOND, START = range(4)
GROUPS = {FIRST: L2_GROUPS[0], LAYER1: L1_GROUPS, SECOND: L2_GROUPS[1], START: START_GROUPS}
SPLIT = {FIRST: L2_SPLIT, LAYER1: L1_SPLIT, SECOND: L2_SPLIT, START: START_SPLIT}
PRODUCTS = {LAYER1: L1_PRODUCTS, START: START_PRODUCTS}
PARTS = 4
NA, NB = len(L2_GROUPS[0]), len(L1_GROUPS)
NG = 2 * NA + NB
SB = sum(n > 0 for n in L1_SPLIT)
NS = 2 * NA + SB
assert NG * PER % RING == 0 and NI1 == 2 * X1_RING and SB % 2 == 0 and NA % 2 == 0 and NP % W2_RING == 0
assert all(len(tiles) >= n <= PARTS // 2 for place in GROUPS for tiles, n in zip(GROUPS[place], SPLIT[place]))


def tiles_of(groups, split, whole):
    return [tile for group, n in zip(groups, split) for tile in (group[:len(group) - n] if whole else group[len(group) - n:])]


L1_WHOLE, L1_PARTS = (tiles_of(L1_GROUPS, L1_SPLIT, whole) for whole in (True, False))
L2_WHOLE, L2_PARTS = (tiles_of(L2_GROUPS[0] + L2_GROUPS[1], L2_SPLIT * 2, whole) for whole in (True, False))
NPARTS = len(L1_PARTS) + len(L2_PARTS)

STEP = [(FIRST, x) for x in range(NA)] + [(LAYER1, x) for x in range(NB)] + [(SECOND, x) for x in range(NA)]
LAST_STEP = [(place, x) for place, x in STEP if place != LAYER1]
START_G = len(START_GROUPS)
START_S = sum(n > 0 for n in START_SPLIT)


def groups_before(c):
    return NG * c + START_G


def splits_before(c):
    return NS * c + START_S


def x2_use(c):
    return NCB * 2 - 1 if isinstance(c, int) and c == NCB - 1 else 2 * c + 2


def x0_use(c):
    return 0 if isinstance(c, int) and c == 0 else 2 * c - 1


def repeat_each(rows, n):
    (step, r), (cs, cols) = rows.ap
    return bass.AP(rows.tensor, rows.offset, [[step, r], [0, n], [cs, cols]])


def repeat_set(rows, n):
    (step, r), (cs, cols) = rows.ap
    return bass.AP(rows.tensor, rows.offset, [[0, n], [step, r], [cs, cols]])


def dlrm_tower(nc, ins, out):
    with ExitStack() as ctx:
        def sb(name, shape, dt=F32):
            return ctx.enter_context(nc.sbuf_tensor(name, shape, dt))

        def ps(name, shape):
            return ctx.enter_context(nc.psum_tensor(name, shape, F32))

        def sem(name):
            return ctx.enter_context(nc.semaphore(name))

        w0 = sb("w0", [P, len(L1_WHOLE), P])
        w1 = sb("w1", [P, len(L2_WHOLE), P])
        w_high = sb("w_high", [P, NPARTS, P], FR)
        w_low = sb("w_low", [P, NPARTS, P], FR)
        w2 = sb("w2", [P, W2_RING, W2_PIECE, P])
        wt3 = sb("wt3", [P, HID2 // P])
        cin_bias = sb("cin_bias", [P, 3])
        bias3_sum = sb("bias3_sum", [P, 1])
        bt1 = sb("bt1", [P, HID1 // P])
        bt2 = sb("bt2", [P, HID2 // P])
        ident = sb("ident", [P, P])
        pair_mask = sb("pair_mask", [P, 2])
        table_rows = sb("table_rows", [P, NCB, NGA], I32)
        first_row = sb("first_row", [P, NGA], I32)
        emb = sb("emb", [P, 2, NGA, EMBED])
        x0 = sb("x0", [FIELDS, COLS])
        x0f = sb("x0f", [P, 2, NJ, COLS])
        x0h = sb("x0h", [P, NI0, COLS])
        x1 = sb("x1", [P, COLS])
        x1h = sb("x1h", [P, X1_RING, COLS])
        prod = sb("prod", [P, RING, GROUP, COLS])
        high = sb("high", [P, PARTS, COLS], FR)
        low = sb("low", [P, PARTS, COLS], FR)
        x2 = sb("x2", [P, COLS])
        x2t = sb("x2t", [P, NCH, MAPS])
        x0d = sb("x0d", [P, 2, NCH, 2, FIELDS])
        gram = sb("gram", [P, FIELDS, BB])
        sums = sb("sums", [P, 3, BATCH])
        staged = gram[:, :, :].rearrange("p f b -> p (f b)")
        parts_raw = staged[:, 0:NPARTS * P].rearrange("p (n o) -> p n o", o=P)
        n_second = len(L1_WHOLE) + len(L1_PARTS) - 2
        w0_second = staged[:, NPARTS * P:(NPARTS + n_second) * P].rearrange("p (n o) -> p n o", o=P)
        wt1 = x0f[:, (NCB - 2) % 2, 0:4, :]
        wt2 = x0f[:, (NCB - 2) % 2, 4:6, :].rearrange("p a n -> p (a n)").rearrange("p (k n) -> p k n", n=HID2)
        dense = x0f[0:EMBED, (NCB - 2) % 2, 6, :]
        hid1 = x0f[:, (NCB - 1) % 2, 0:4, :]
        hid2 = x0f[:, (NCB - 1) % 2, 4:6, :]
        y = x0f[:, (NCB - 1) % 2, 6, :]
        x0_dram = nc.dram_tensor("x0_dram", (NCB, FIELDS, COLS), F32, kind="Internal").ap()

        l1_ps = ps("l1_ps", [P, COLS])
        l2_ps = ps("l2_ps", [P, 2, COLS])
        t_ps = ps("t_ps", [P, COLS])
        g_ps = ps("g_ps", [P, 4, COLS])
        hid1_ps = [l1_ps[:, :], l2_ps[:, (NCB - 2) % 2, :], g_ps[:, 1, :], g_ps[:, 2, :]]
        hid2_ps = [g_ps[:, 3, :], l2_ps[:, (NCB - 1) % 2, :]]

        ids_in, rows_ready = sem("ids_in"), sem("rows_ready")
        ident_in, mask_in, bias_in = sem("ident_in"), sem("mask_in"), sem("bias_in")
        w0_in, w1_in, parts_in, mlp_in = sem("w0_in"), sem("w1_in"), sem("parts_in"), sem("mlp_in")
        w0_folded, w_high_ready, w_low_ready = sem("w0_folded"), sem("w_high_ready"), sem("w_low_ready")
        gathered = [sem(f"gathered{r}") for r in range(2)]
        gathered0 = [sem(f"gathered0_{v}") for v in range(4)]
        bank_filled, bank_copied = sem("bank_filled"), sem("bank_copied")
        x0_stored, x0_in, x0_rows_in = sem("x0_stored"), sem("x0_in"), sem("x0_rows_in")
        x1h_in = [sem(f"x1h_in{r}") for r in range(X1_RING)]
        prod_ready, prod_used = sem("prod_ready"), sem("prod_used")
        high_ready, low_ready, split_used = sem("high_ready"), sem("low_ready"), sem("split_used")
        x1_ready, x2_ready = sem("x1_ready"), sem("x2_ready")
        sum1_done, sum2_done = sem("sum1_done"), sem("sum2_done")
        sum3_done = sem("sum3_done")
        gram_ps_done, gram_copied = sem("gram_ps_done"), sem("gram_copied")
        w2_in = [sem(f"w2_in{r}") for r in range(W2_RING)]
        w2_used = sem("w2_used")
        mlp_ps_done, mlp_ready = sem("mlp_ps_done"), sem("mlp_ready")
        out_written = sem("out_written")

        def walk(eng, step):
            for k in range(2):
                step(0, k, k)
            with eng.Fori(0, NBB - 1) as t:
                for k in range(2, PER + 2):
                    step(t, k, t * PER + k)
            for k in range(2, PER):
                step(NBB - 1, k, PER * (NBB - 1) + k)

        def layer3_pieces(k, c, place, x):
            if isinstance(c, int):
                return ()
            if k == PER and place == SECOND and x >= NA - 2:
                return (x - NA + 2,)
            if k == PER + 1 and place == FIRST:
                return (x + 2,)
            if k == PER + 1 and place == LAYER1:
                return (NA + 2 + x,) if x < NB - 1 else range(NA + 1 + NB, NP)
            return ()

        def is_last(c):
            return isinstance(c, int) and c == NCB - 1

        def groups(k, c):
            split = 0
            for n, (place, x) in enumerate(LAST_STEP if is_last(c) else STEP):
                yield n, place, x, (START_G + NG * k + n) % RING, split
                split += SPLIT[place][x] > 0

        def part_slots(place, x):
            at = PARTS // 2 * (sum(n > 0 for n in SPLIT[place][:x]) % 2)
            return slice(at, at + SPLIT[place][x])

        block = ctx.enter_context(nc.Block())

        @block.gpsimd
        def _(pool):
            def lookup(c, b, g, done):
                nc.gpsimd.indirect_dma_start(
                    out=emb[:, b, g, :], out_offset=None, in_=ins["table"],
                    in_offset=bass.IndirectOffsetOnAxis(ap=table_rows[:, c, g:g + 1].bitcast(U32), axis=0)).then_inc(done, 16)

            pool.wait_ge(rows_ready, 1)
            for c in range(NCB):
                if c >= 2:
                    pool.wait_ge(x0_stored, 16 * (c + 2))
                for g in range(NGA):
                    lookup(c, c % 2, g, gathered[c % 2] if c else gathered0[g // QG])

        @block.sync
        def _(sp):
            sp.dma_start(table_rows[:, :, :], ins["ids"]).then_inc(ids_in, 16)
            sp.dma_start(first_row[:, :], ins["first_row"]).then_inc(ids_in, 16)
            sp.dma_start(ident[:, :], ins["ident"]).then_inc(ident_in, 16)
            sp.dma_start(w0[:, :, :], ins["w0_first"][:, 0:len(L1_WHOLE), :]).then_inc(w0_in, 16)
            sp.dma_start(parts_raw[:, 0:len(L1_PARTS), :], ins["w0_first"][:, len(L1_WHOLE):, :]).then_inc(w0_in, 16)
            sp.dma_start(w0_second, ins["w0_second"]).then_inc(w0_in, 16)
            sp.dma_start(cin_bias[:, :], ins["cin_bias"]).then_inc(bias_in, 16)

            def store_x0(c, b, g, n):
                sp.dma_start(x0_dram[c, GF * g:GF * (g + n), :].rearrange("(g l) (b d) -> l b g d", l=GF, d=EMBED),
                             emb[:, b, g:g + n, :]).then_inc(x0_stored, 16)

            def load_x0h(c, i):
                sp.dma_start(x0h[:, i, :], repeat_each(x0_dram[c, HT * i:HT * (i + 1), :], FT)).then_inc(x0_in, 16)

            def load_x0f(c, b, j):
                sp.dma_start(x0f[:, b, j, :], repeat_set(x0_dram[c, FT * j:FT * (j + 1), :], HT)).then_inc(x0_in, 16)

            def load_x1(i):
                sp.dma_start(x1h[:, i % X1_RING, :],
                             repeat_each(x1[HT * i:HT * (i + 1), :], FT)).then_inc(x1h_in[i % X1_RING], 16)

            def load_w2(n):
                sp.dma_start(w2[:, n % W2_RING, :, :],
                             ins["w2"][:, n * W2_PIECE:(n + 1) * W2_PIECE, :]).then_inc(w2_in[n % W2_RING], 16)

            def refill_w2(t, first, end):
                for n in range(first, end):
                    sp.wait_ge(w2_used, t * NP + n + 1)
                    load_w2((n + W2_RING) % NP)

            for v in range(4):
                sp.wait_ge(gathered0[v], 16 * QG)
                store_x0(0, 0, QG * v, QG)
                if v:
                    sp.wait_ge(x0_in, 16 * 3 * v)
                sp.wait_ge(x0_stored, 16 * (v + 1))
                load_x0h(0, v)
                load_x0f(0, 0, 2 * v)
                load_x0f(0, 0, 2 * v + 1)
            sp.dma_start(x0[:, :], x0_dram[0]).then_inc(x0_rows_in, 16)
            sp.dma_start(pair_mask[:, :], ins["pair_mask"]).then_inc(mask_in, 16)
            sp.dma_start(parts_raw[:, len(L1_PARTS):, :], ins["w1_parts"]).then_inc(parts_in, 16)
            sp.dma_start(w1[:, :, :], ins["w1_whole"]).then_inc(w1_in, 16)
            sp.wait_ge(gathered[1], 16 * NGA)
            store_x0(1, 1, 0, NGA)
            for n in range(W2_RING):
                load_w2(n)
            sp.wait_ge(x1_ready, 1)
            for i in range(X1_RING):
                load_x1(i)

            def step(t, k, c):
                has_layer3 = k == PER + 1
                if not is_last(c):
                    if k == 0:
                        sp.wait_ge(prod_ready, START_G)
                    sp.wait_ge(x0_stored, 16 * (c + 5))
                    for i in range(NI0):
                        load_x0h(c + 1, i)
                    for j in range(NJ):
                        load_x0f(c + 1, (k + 1) % 2, j)
                    sp.wait_ge(bank_filled, x0_use(c) + 1)
                    sp.dma_start(x0[:, :], x0_dram[c + 1]).then_inc(x0_rows_in, 16)
                for i in range(X1_RING):
                    sp.wait_ge(prod_ready, groups_before(c) + 2 * i + 2)
                    load_x1(X1_RING + i)
                    if has_layer3:
                        refill_w2(t, 2 * i, 2 * i + 2)
                if has_layer3:
                    refill_w2(t, 2 * X1_RING, NP)
                if is_last(c):
                    sp.dma_start(wt1[:, 0:3, :], ins["wt1"][0:3 * P, :].rearrange("(k p) n -> p k n", p=P)).then_inc(mlp_in, 16)
                    sp.dma_start(wt1[0:EMBED, 3, :], ins["wt1"][3 * P:3 * P + EMBED, :]).then_inc(mlp_in, 16)
                    sp.dma_start(wt2, ins["wt2"].rearrange("(k p) n -> p k n", p=P)).then_inc(mlp_in, 16)
                    sp.dma_start(dense, ins["dense"]).then_inc(mlp_in, 16)
                    sp.dma_start(wt3[:, :], ins["wt3"]).then_inc(mlp_in, 16)
                    sp.dma_start(bt1[:, :], ins["bt1"]).then_inc(mlp_in, 16)
                    sp.dma_start(bt2[:, :], ins["bt2"]).then_inc(mlp_in, 16)
                    return
                if not isinstance(c, int) or c < NCB - 2:
                    sp.wait_ge(gathered[k % 2], 16 * NGA * (PER // 2 * t + (k + 2 + k % 2) // 2))
                    store_x0(c + 2, k % 2, 0, NGA)
                sp.wait_ge(sum1_done, c + 2)
                load_x1(0)
                load_x1(1)
                for i in range(2, X1_RING):
                    sp.wait_ge(prod_ready, groups_before(c) + NA + NB + 2 * i + 2)
                    load_x1(i)

            walk(sp, step)
            refill_w2(NBB - 1, 0, NP - W2_RING)
            sp.wait_ge(mlp_ready, 7)
            sp.dma_start(out.rearrange("b a -> a b"), y[0:1, :]).then_inc(out_written, 16)
            sp.wait_ge(out_written, 16)

        @block.vector
        def _(dve):
            dve.wait_ge(ids_in, 32)
            nc.vector.tensor_tensor(table_rows[:, :, :], table_rows[:, :, :], first_row[:, :].unsqueeze(1).to_broadcast([P, NCB, NGA]),
                                    ALU.add).then_inc(rows_ready, 1)
            dve.wait_ge(w0_in, 16 * 3)
            n = 0
            for home, tiles in ((w0, L1_WHOLE), (parts_raw, L1_PARTS)):
                for at, (i, j) in enumerate(tiles):
                    if i == PAIR:
                        continue
                    rows = slice(HALF if j == 2 * i else 0, P)
                    nc.vector.tensor_tensor(home[rows, at, :], home[rows, at, :], w0_second[rows, n, :],
                                            ALU.add).then_inc(w0_folded, 1)
                    n += 1

            def weights_low(layer2):
                a, b = (len(L1_PARTS), NPARTS) if layer2 else (0, len(L1_PARTS))
                dve.wait_ge(w_high_ready, 1 + layer2)
                nc.vector.tensor_tensor(w_low[:, a:b, :], parts_raw[:, a:b, :], w_high[:, a:b, :].bitcast(F32),
                                        ALU.subtract).then_inc(w_low_ready, 1)

            def product(place, x, g, lows, buf, b):
                if not (isinstance(g, int) and g < RING):
                    dve.wait_ge(prod_used, g - (RING - 1))
                if not (isinstance(lows, int) and lows == 0):
                    dve.wait_ge(low_ready, lows)
                if place in PRODUCTS:
                    parts = [(prod[:, buf, s:s + n, :], x0h[:, i, :].unsqueeze(1).to_broadcast([P, n, COLS]),
                              x0f[:, b, j:j + (n - 1) * step + 1:step, :]) for s, i, j, step, n in PRODUCTS[place][x]]
                    for s, (kind, i) in enumerate(GROUPS[place][x]):
                        if kind == PAIR:
                            for rows, e in ((slice(HALF, P), i), (slice(0, HALF), i + 1)):
                                parts.append((prod[rows, buf, s, :], x0h[HALF:P, e, :], x0f[HALF:P, b, 2 * e + 1, :]))
                else:
                    i, j = GROUPS[place][x][0]
                    parts = [(prod[:, buf, :, :], x1h[:, i % X1_RING, :].unsqueeze(1).to_broadcast([P, GROUP, COLS]),
                              x0f[:, b, j:j + GROUP, :])]
                for to, left, right in parts:
                    made = nc.vector.tensor_tensor(to, left, right, ALU.mult)
                made.then_inc(prod_ready, 1)

            def low_part(place, x, split, buf):
                count = SPLIT[place][x]
                slots = part_slots(place, x)
                dve.wait_ge(high_ready, split + 1)
                nc.vector.tensor_tensor(low[:, slots, :], prod[:, buf, len(GROUPS[place][x]) - count:len(GROUPS[place][x]), :],
                                        high[:, slots, :].bitcast(F32), ALU.subtract).then_inc(low_ready, 1)

            def sum_dims(x, layer, c, done):
                nc.vector.tensor_reduce(sums[:, layer, bass.ds(c * CB, CB)],
                                        x[:, :].rearrange("p (b d) -> p b d", d=EMBED), AX.X, ALU.add).then_inc(done, 1)

            split = 0
            for x in range(START_G):
                if START_QUARTER.index(START_QUARTER[x]) == x:
                    dve.wait_ge(x0_in, 16 * 3 * (START_QUARTER[x] + 1))
                if START_QUARTER[x] == 3 and START_QUARTER[x - 1] < 3:
                    weights_low(0)
                product(START, x, x, sum(n > 0 for n in START_SPLIT[:max(x - RING + 1, 0)]), x % RING, 0)
                if x and START_SPLIT[x - 1]:
                    low_part(START, x - 1, split, (x - 1) % RING)
                    split += 1
            weights_low(1)
            dve.wait_ge(x1_ready, 1)
            sum_dims(x1, 0, 0, sum1_done)

            def step(t, k, c):
                g0, s0 = groups_before(c), splits_before(c)
                earlier = []
                for n, place, x, buf, split in groups(k, c):
                    if place != LAYER1 and x % 2 == 0:
                        dve.wait_ge(x1h_in[x // 2], 16 * (2 * c + (1 if place == FIRST else 2)))
                    if (place, x) == (LAYER1, 0):
                        dve.wait_ge(x0_in, 16 * X0_DMAS * (c + 2))
                    if n >= RING:
                        lows = s0 + earlier[n - RING]
                    elif k:
                        lows = s0 - (RING - 1) + n
                    else:
                        lows = min(s0, s0 - RING + 2 + n)
                    product(place, x, g0 + n, lows, buf, (k + 1) % 2 if place == LAYER1 else k % 2)
                    if n == 0:
                        if k:
                            low_part(SECOND, NA - 1, s0 - 1, (START_G + NG * k - 1) % RING)
                    elif SPLIT[last[0]][last[1]]:
                        low_part(last[0], last[1], s0 + last[3], last[2])
                    last = (place, x, buf, split)
                    earlier.append(split + (SPLIT[place][x] > 0))
                    if k and (place, x) == (FIRST, 5):
                        dve.wait_ge(x2_ready, c)
                        sum_dims(x2, 1, c - 1, sum2_done)
                    if not is_last(c) and (place, x) == (SECOND, 3):
                        dve.wait_ge(x1_ready, c + 2)
                        sum_dims(x1, 0, c + 1, sum1_done)

            walk(dve, step)
            g_last = groups_before(NCB) - NB - 1
            low_part(SECOND, NA - 1, splits_before(NCB) - SB - 1, g_last % RING)
            dve.wait_ge(x2_ready, NCB)
            sum_dims(x2, 1, NCB - 1, sum2_done)

        @block.scalar
        def _(act):
            act.wait_ge(w0_folded, n_second)
            nc.scalar.activation(w_high[:, 0:len(L1_PARTS), :], parts_raw[:, 0:len(L1_PARTS), :],
                                 ACT.Copy).then_inc(w_high_ready, 1)
            act.wait_ge(bias_in, 16)
            nc.scalar.mul(bias3_sum[:, :], cin_bias[:, 2:3], float(EMBED)).then_inc(sum3_done, 1)

            def high_part(place, x, g, split, buf):
                count = SPLIT[place][x]
                slots = part_slots(place, x)
                if not (isinstance(split, int) and split < 2):
                    act.wait_ge(split_used, split - 1)
                act.wait_ge(prod_ready, g + 1)
                nc.scalar.activation(high[:, slots, :],
                                     prod[:, buf, len(GROUPS[place][x]) - count:len(GROUPS[place][x]), :],
                                     ACT.Copy).then_inc(high_ready, 1)

            def x0_diagonal(c, b):
                act.wait_ge(bank_filled, x0_use(c) + 1)
                for a in range(2):
                    made = nc.scalar.mul(x0d[:, b, :, a, :], t_ps[:, 0:NCH * FIELDS].rearrange("p (n f) -> p n f", f=FIELDS),
                                         pair_mask[:, a:a + 1])
                made.then_inc(bank_copied, 1)

            def store_x1():
                nc.scalar.activation(x1[:, :], l1_ps[:, :], ACT.Identity, bias=cin_bias[:, 0:1]).then_inc(x1_ready, 1)

            def store_x2(c, b):
                act.wait_ge(split_used, splits_before(c) + NS - SB * is_last(c))
                nc.scalar.activation(x2[:, :], l2_ps[:, b, :], ACT.Identity,
                                     bias=cin_bias[:, 1:2]).then_inc(x2_ready, 1)

            def store_x2t(c):
                act.wait_ge(bank_filled, x2_use(c) + 1)
                nc.scalar.activation(x2t[:, :, :].rearrange("p n h -> p (n h)"), t_ps[:, :],
                                     ACT.Copy).then_inc(bank_copied, 1)

            def store_gram(c, q, r):
                if r == 0:
                    act.wait_ge(gram_ps_done, c + 1)
                to = gram[:, :, q * CB:(q + 1) * CB].rearrange("h f (n r a) -> h r n a f", n=NCH, r=4)[:, r]
                nc.scalar.activation(to, g_ps[:, r, :].rearrange("h (n a f) -> h n a f", n=NCH, a=2),
                                     ACT.Copy).then_inc(gram_copied, 1)

            def store_sum3(t):
                act.wait_ge(sum3_done, t + 1)
                act.wait_ge(w2_used, NP * t + NP)
                nc.scalar.activation(sums[:, 2, bass.ds(t * BB, BB)], g_ps[:, 0, 0:BB], ACT.Identity,
                                     bias=bias3_sum[:, 0:1]).then_inc(sum3_done, 1)

            split = 0
            for x, count in enumerate(START_SPLIT):
                if count:
                    high_part(START, x, x, split, x % RING)
                    split += 1
            act.wait_ge(parts_in, 16)
            nc.scalar.activation(w_high[:, len(L1_PARTS):, :], parts_raw[:, len(L1_PARTS):, :],
                                 ACT.Copy).then_inc(w_high_ready, 1)
            act.wait_ge(mask_in, 16)
            x0_diagonal(0, 0)
            act.wait_ge(prod_used, START_G)
            store_x1()

            def step(t, k, c):
                g0, s0 = groups_before(c), splits_before(c)
                for n, place, x, buf, split in groups(k, c):
                    if SPLIT[place][x]:
                        high_part(place, x, g0 + n, s0 + split, buf)
                    if k and (place, x) == (FIRST, 0):
                        store_x2(c - 1, (k - 1) % 2)
                    if k and (place, x) == ((SECOND, 0) if is_last(c) else (LAYER1, 0)):
                        store_x2t(c - 1)
                    if k == PER + 1 and (place, x) == (SECOND, 0):
                        store_sum3(t)
                    if not is_last(c) and (place, x) == (SECOND, 0):
                        for r in range(X1_RING):
                            act.wait_ge(x1h_in[r], 16 * (2 * c + 2))
                        act.wait_ge(sum1_done, c + 1)
                        act.wait_ge(prod_used, g0 + NA + NB)
                        store_x1()
                    if k and place == SECOND and x in (4, 5):
                        for r in range(2):
                            store_gram(c - 1, (k - 1) % PER, 2 * (x - 4) + r)
                    if not is_last(c) and (place, x) == (SECOND, 6):
                        x0_diagonal(c + 1, (k + 1) % 2)

            walk(act, step)
            store_x2(NCB - 1, (NCB - 1) % 2)
            store_x2t(NCB - 1)
            for r in range(4):
                store_gram(NCB - 1, PER - 1, r)
            store_sum3(NBB - 1)
            act.wait_ge(mlp_in, 16 * 7)
            for m in range(HID1 // P):
                act.wait_ge(mlp_ps_done, m + 1)
                nc.scalar.activation(hid1[:, m, :], hid1_ps[m], ACT.Relu, bias=bt1[:, m:m + 1]).then_inc(mlp_ready, 1)
            for m in range(HID2 // P):
                act.wait_ge(mlp_ps_done, HID1 // P + m + 1)
                nc.scalar.activation(hid2[:, m, :], hid2_ps[m], ACT.Relu, bias=bt2[:, m:m + 1]).then_inc(mlp_ready, 1)
            act.wait_ge(mlp_ps_done, HID1 // P + HID2 // P + 1)
            nc.scalar.activation(y[0:1, :], t_ps[0:1, :], ACT.Copy).then_inc(mlp_ready, 1)

        @block.tensor
        def _(pe):
            def wait_bank(n):
                if not (isinstance(n, int) and n == 0):
                    pe.wait_ge(bank_copied, n)

            def turn(to, rows, n):
                a, m = rows.base_partition(), rows.partition_size()
                unit = ident[a:a + m, a:a + m]
                if n == 0:
                    return nc.tensor.matmul(to, rows, unit, start=True, stop=True)
                return nc.tensor.transpose(to, rows, unit)

            def transpose_x0(c):
                pe.wait_ge(x0_rows_in, 16 * (c + 1))
                wait_bank(x0_use(c))
                for n in range(NCH):
                    mm = turn(t_ps[:, n * FIELDS:(n + 1) * FIELDS], x0[:, n * P:(n + 1) * P], n)
                mm.then_inc(bank_filled, 1)

            def contract(place, x, g, split, buf, acc):
                tiles, count = GROUPS[place][x], SPLIT[place][x]
                start = (place, x) in ((FIRST, 0), (LAYER1, 0), (START, 0))
                stop = (place, x) in ((SECOND, NA - 1), (LAYER1, NB - 1), (START, len(START_GROUPS) - 1))
                layer1 = place in PRODUCTS
                pe.wait_ge(prod_ready, g + 1)
                for n, tile in enumerate(tiles[:len(tiles) - count]):
                    weights = w0[:, L1_WHOLE.index(tile), :] if layer1 else w1[:, L2_WHOLE.index(tile), :]
                    mm = nc.tensor.matmul(acc, weights, prod[:, buf, n, :], start=start and n == 0,
                                          stop=stop and not count and n == len(tiles) - 1)
                if count < len(tiles):
                    mm.then_inc(prod_used, 1)
                if not count:
                    return
                pe.wait_ge(high_ready, split + 1)
                slots = part_slots(place, x)
                parts = L1_PARTS if layer1 else L2_PARTS
                ats = [(0 if layer1 else len(L1_PARTS)) + parts.index(tile) for tile in tiles[len(tiles) - count:]]
                for n, at in enumerate(ats):
                    mm = nc.tensor.matmul(acc, w_high[:, at, :], high[:, slots.start + n, :], start=False, stop=False)
                    if n == 0 and count == len(tiles):
                        mm.then_inc(prod_used, 1)
                    nc.tensor.matmul(acc, w_low[:, at, :], high[:, slots.start + n, :], start=False, stop=False)
                pe.wait_ge(low_ready, split + 1)
                for n, at in enumerate(ats):
                    mm = nc.tensor.matmul(acc, w_high[:, at, :], low[:, slots.start + n, :], start=False,
                                          stop=stop and n == count - 1)
                mm.then_inc(split_used, 1)

            def transpose_x2(c):
                pe.wait_ge(x2_ready, c + 1)
                wait_bank(x2_use(c))
                for n in range(NCH):
                    mm = nc.tensor.transpose(t_ps[:, n * P:(n + 1) * P], x2[:, n * P:(n + 1) * P], ident[:, :])
                mm.then_inc(bank_filled, 1)

            def make_gram(c, b, n):
                if n == 0:
                    wait_bank(x2_use(c) + 1)
                for r in range(4):
                    rows = slice(32 * r, 32 * r + 32)
                    mm = nc.tensor.matmul(g_ps[:, r, n * P:(n + 1) * P], x2t[rows, n, :],
                                          x0d[rows, b, n, :, :].rearrange("p a f -> p (a f)"), start=True, stop=True)
                if n == NCH - 1:
                    mm.then_inc(gram_ps_done, 1)

            def layer3(t, n):
                pe.wait_ge(w2_in[n % W2_RING], 16 * (NP // W2_RING * t + n // W2_RING + 1))
                for e in range(W2_PIECE):
                    f = n * W2_PIECE + e
                    mm = nc.tensor.matmul(g_ps[:, 0, 0:BB], w2[:, n % W2_RING, e, :], gram[:, f, :],
                                          start=f == 0, stop=f == FIELDS - 1)
                mm.then_inc(w2_used, 1)

            pe.wait_ge(ident_in, 16)
            pe.wait_ge(w0_folded, n_second)
            split = 0
            for x in range(START_G):
                if x == START_QUARTER.index(3):
                    pe.wait_ge(w_low_ready, 1)
                contract(START, x, x, split, x % RING, l1_ps[:, :])
                split += START_SPLIT[x] > 0
            transpose_x0(0)
            pe.wait_ge(w1_in, 16)
            pe.wait_ge(w_low_ready, 2)

            def step(t, k, c):
                g0, s0 = groups_before(c), splits_before(c)
                for n, place, x, buf, split in groups(k, c):
                    if (place, x) == (LAYER1, 0):
                        pe.wait_ge(x1_ready, c + 1)
                    if place == LAYER1:
                        contract(place, x, g0 + n, s0 + split, buf, l1_ps[:, :])
                    else:
                        contract(place, x, g0 + n, s0 + split, buf, l2_ps[:, k % 2, :])
                    if k and (place, x) == (FIRST, NA - 1):
                        transpose_x2(c - 1)
                    if k and place == SECOND and x < NCH:
                        if k == PER + 1 and x == 0:
                            pe.wait_ge(sum3_done, t + 2)
                        make_gram(c - 1, (k - 1) % 2, x)
                    if not is_last(c) and (place, x) == (SECOND, NCH):
                        transpose_x0(c + 1)
                    for n in layer3_pieces(k, c, place, x):
                        if n == 0:
                            pe.wait_ge(gram_copied, 4 * c)
                        layer3(t, n)
                if k:
                    pe.wait_ge(x2_ready, c)

            walk(pe, step)

            def hidden1(m, n, start=False, stop=False):
                rows, rhs = (P, sums[:, n, :]) if n < 3 else (EMBED, dense)
                mm = nc.tensor.matmul(hid1_ps[m], wt1[0:rows, n, m * P:(m + 1) * P], rhs, start=start, stop=stop)
                if stop:
                    mm.then_inc(mlp_ps_done, 1)

            pe.wait_ge(mlp_in, 16 * 7)
            pe.wait_ge(sum1_done, NCB)
            pe.wait_ge(x1_ready, NCB)
            hidden1(0, 0, start=True)
            hidden1(0, 3)
            transpose_x2(NCB - 1)
            hidden1(1, 0, start=True)
            hidden1(1, 3)
            for n in range(NCH):
                make_gram(NCB - 1, (NCB - 1) % 2, n)
            pe.wait_ge(sum2_done, NCB)
            hidden1(0, 1)
            hidden1(1, 1)
            pe.wait_ge(gram_copied, 4 * NCB)
            for n in range(NP):
                layer3(NBB - 1, n)
            for m in range(2, 4):
                for n in (0, 3, 1):
                    hidden1(m, n, start=n == 0)
            pe.wait_ge(sum3_done, NBB + 1)
            for m in range(HID1 // P):
                hidden1(m, 2, stop=True)
            for n in range(HID1 // P):
                pe.wait_ge(mlp_ready, n + 1)
                for m in range(HID2 // P):
                    mm = nc.tensor.matmul(hid2_ps[m], wt2[:, n, m * P:(m + 1) * P], hid1[:, n, :],
                                          start=n == 0, stop=n == HID1 // P - 1)
                    if n == HID1 // P - 1:
                        mm.then_inc(mlp_ps_done, 1)
            for n in range(HID2 // P):
                pe.wait_ge(mlp_ready, HID1 // P + n + 1)
                mm = nc.tensor.matmul(t_ps[0:1, :], wt3[:, n:n + 1], hid2[:, n, :], start=n == 0, stop=n == HID2 // P - 1)
            mm.then_inc(mlp_ps_done, 1)


def kernel(**inputs):
    import numpy as np
    import concourse.bacc as bacc
    from concourse.bass_utils import run_bass_kernel_spmd

    a = {name: np.asarray(value) for name, value in inputs.items()}
    w0, w1, w2 = a["L0_rec_W0"], a["L0_rec_W1"], a["L0_rec_W2"]
    w0_hf = w0.reshape(MAPS, NI0, HT, NJ, FT).transpose(1, 3, 2, 4, 0).reshape(NI0, NJ, P, MAPS)
    w0_fh = w0.reshape(MAPS, NJ, FT, NI0, HT).transpose(3, 1, 4, 2, 0).reshape(NI0, NJ, P, MAPS)
    w1_hf = w1.reshape(MAPS, NI1, HT, NJ, FT).transpose(1, 3, 2, 4, 0).reshape(NI1, NJ, P, MAPS)

    def w0_tile(i, j):
        if i == PAIR:
            return np.concatenate([w0_hf[j + 1, 2 * j + 3, HALF:], w0_hf[j, 2 * j + 1, HALF:]])
        return w0_hf[i, j]

    tables = [a[f"tbl_{f}"] for f in range(FIELDS)]
    first_row = np.cumsum([0] + [x.shape[0] for x in tables[:-1]]).astype(np.int32)
    l1_tiles = L1_WHOLE + L1_PARTS
    arrays = {
        "table": np.concatenate(tables),
        "first_row": np.repeat(first_row.reshape(NGA, GF).T, CB, axis=0),
        "ids": a["ids"].reshape(NCB, CB, NGA, GF).transpose(3, 1, 0, 2).reshape(P, NCB, NGA),
        "dense": a["dense_ctx"].T,
        "w0_first": np.stack([w0_tile(i, j) for i, j in l1_tiles], axis=1),
        "w0_second": np.stack([w0_fh[i, j] for i, j in l1_tiles if i != PAIR], axis=1),
        "w1_whole": np.stack([w1_hf[i, j] for i, j in L2_WHOLE], axis=1),
        "w1_parts": np.stack([w1_hf[i, j] for i, j in L2_PARTS], axis=1),
        "w2": w2.reshape(MAPS, MAPS, FIELDS).transpose(1, 2, 0),
        "cin_bias": np.stack([a["L0_rec_b0"], a["L0_rec_b1"], a["L0_rec_b2"]], axis=1),
        "wt1": a["W_top1"], "wt2": a["W_top2"],
        "wt3": a["W_top3"].reshape(HID2 // P, P).T,
        "bt1": a["b_top1"].reshape(HID1 // P, P).T,
        "bt2": a["b_top2"].reshape(HID2 // P, P).T,
        "ident": np.eye(P, dtype=np.float32),
        "pair_mask": (np.arange(P)[:, None] // EMBED % 2 == np.arange(2)).astype(np.float32),
    }
    arrays = {name: np.ascontiguousarray(x) for name, x in arrays.items()}

    nc = bacc.Bacc("TRN2", target_bir_lowering=False, num_devices=1)
    aps = {name: nc.dram_tensor(f"in_{name}", x.shape, mybir.dt.from_np(x.dtype), kind="ExternalInput").ap()
           for name, x in arrays.items()}
    out = nc.dram_tensor("out", (BATCH, 1), F32, kind="ExternalOutput").ap()
    dlrm_tower(nc, aps, out)
    r = run_bass_kernel_spmd(nc, [{f"in_{name}": x for name, x in arrays.items()}], core_ids=[0])
    return r.results[0]["out"]
```
